# Optimizing a Trainium2 kernel written in Bass

```python
import numpy as np
import jax
import jax.numpy as jnp

def _softmax(x, axis=-1):
    return jax.nn.softmax(x, axis=axis)

def _gelu(x):
    return jax.nn.gelu(x, approximate=True)

def _silu(x):
    return jax.nn.silu(x)

def _sigmoid(x):
    return jax.nn.sigmoid(x)

def _layernorm(x, axis=-1, eps=1e-05):
    m = jnp.mean(x, axis=axis, keepdims=True)
    v = jnp.var(x, axis=axis, keepdims=True)
    return (x - m) / jnp.sqrt(v + eps)

def _scatter_add(tgt, idx, src, axis=0):
    return tgt.at[idx].add(src)

def _segment_sum(src, seg, n):
    return jax.ops.segment_sum(src, seg, n)
kernel_name = 'mk_metaformer_d1_conv_nhwc128_r4_08b6ea'

def setup_inputs(seed: int=0):
    np.random.seed(seed)
    _w = jnp.asarray

    def _rec_inputs():
        import jax
        import jax.numpy as jnp
        _gk = jax.random.key(seed)
        x = -0.000125 + 0.9999 * jax.random.normal(jax.random.fold_in(_gk, 1), (1, 128, 128, 32), jnp.float32)
        return x
    x = _rec_inputs()

    def _L0_conv_setup():
        import jax, jax.numpy as jnp
        import numpy as np
        D_PAIR = 32
        C = 32
        LN_EPS = 1e-05

        def _layernorm(x, w, b):
            m = jnp.mean(x, axis=-1, keepdims=True)
            v = jnp.var(x, axis=-1, keepdims=True)
            return (x - m) * jax.lax.rsqrt(v + LN_EPS) * w + b
        key = jax.random.key(seed)
        ks = jax.random.split(key, 12)
        B, N = (1, 128)
        Z_raw = jax.random.normal(ks[0], (B, N, N, D_PAIR), dtype=jnp.float32)
        Z_mask_row = jnp.ones((B, N, N), dtype=jnp.float32)
        s = 1.0 / np.sqrt(D_PAIR)
        return {'Z_raw': Z_raw, 'Z_mask_row': Z_mask_row, 'ln1_w': jnp.ones((D_PAIR,), jnp.float32), 'ln1_b': jnp.zeros((D_PAIR,), jnp.float32), 'lrp_w': jax.random.normal(ks[1], (2 * C, D_PAIR), jnp.float32) * s, 'lrp_b': jnp.zeros((2 * C,), jnp.float32), 'gate_w': jax.random.normal(ks[2], (2 * C, D_PAIR), jnp.float32) * (0.02 * s), 'gate_b': jnp.ones((2 * C,), jnp.float32), 'og_w': jax.random.normal(ks[3], (D_PAIR, D_PAIR), jnp.float32) * (0.02 * s), 'og_b': jnp.ones((D_PAIR,), jnp.float32), 'ln2_w': jnp.ones((C,), jnp.float32), 'ln2_b': jnp.zeros((C,), jnp.float32), 'op_w': jax.random.normal(ks[4], (D_PAIR, D_PAIR), jnp.float32) * (0.02 * s), 'out_bias': jnp.zeros((D_PAIR,), jnp.float32)}
    _L0_conv_all = _L0_conv_setup()
    _L0_conv_in = {k: v for k, v in _L0_conv_all.items() if k in ('Z_mask_row', 'ln1_w', 'ln1_b', 'lrp_w', 'lrp_b', 'gate_w', 'gate_b', 'og_w', 'og_b', 'ln2_w', 'ln2_b', 'op_w', 'out_bias')}
    del _L0_conv_all

    def _L0_ffn_setup():
        import jax, jax.numpy as jnp
        import numpy as np
        B, N, D, C, E, K = (8, 2048, 32, 32, 8, 2)
        key = jax.random.key(seed)
        k0, k1, k2 = jax.random.split(key, 3)
        x = jax.random.normal(k0, (B, N, D), dtype=jnp.float32)
        router_w = jax.random.normal(k1, (D, E), dtype=jnp.float32) * 0.05
        router_b = jnp.zeros((E,), dtype=jnp.float32)
        expert_w = jax.random.normal(k2, (E, D, C), dtype=jnp.float32) * (1.0 / np.sqrt(D))
        expert_b = jnp.zeros((E, C), dtype=jnp.float32)
        return {'x': x, 'router_w': router_w, 'router_b': router_b, 'expert_w': expert_w, 'expert_b': expert_b}
    _L0_ffn_all = _L0_ffn_setup()
    _L0_ffn_in = {k: v for k, v in _L0_ffn_all.items() if k in ('router_w', 'router_b', 'expert_w', 'expert_b')}
    del _L0_ffn_all
    return {'x': x, 'L0_conv_Z_mask_row': _L0_conv_in['Z_mask_row'], 'L0_conv_ln1_w': _L0_conv_in['ln1_w'], 'L0_conv_ln1_b': _L0_conv_in['ln1_b'], 'L0_conv_lrp_w': _L0_conv_in['lrp_w'], 'L0_conv_lrp_b': _L0_conv_in['lrp_b'], 'L0_conv_gate_w': _L0_conv_in['gate_w'], 'L0_conv_gate_b': _L0_conv_in['gate_b'], 'L0_conv_og_w': _L0_conv_in['og_w'], 'L0_conv_og_b': _L0_conv_in['og_b'], 'L0_conv_ln2_w': _L0_conv_in['ln2_w'], 'L0_conv_ln2_b': _L0_conv_in['ln2_b'], 'L0_conv_op_w': _L0_conv_in['op_w'], 'L0_conv_out_bias': _L0_conv_in['out_bias'], 'L0_ffn_router_w': _L0_ffn_in['router_w'], 'L0_ffn_router_b': _L0_ffn_in['router_b'], 'L0_ffn_expert_w': _L0_ffn_in['expert_w'], 'L0_ffn_expert_b': _L0_ffn_in['expert_b']}

def reference(x, L0_conv_Z_mask_row, L0_conv_ln1_w, L0_conv_ln1_b, L0_conv_lrp_w, L0_conv_lrp_b, L0_conv_gate_w, L0_conv_gate_b, L0_conv_og_w, L0_conv_og_b, L0_conv_ln2_w, L0_conv_ln2_b, L0_conv_op_w, L0_conv_out_bias, L0_ffn_router_w, L0_ffn_router_b, L0_ffn_expert_w, L0_ffn_expert_b):
    import jax
    import jax.numpy as jnp

    def _L0_conv_ref(Z_raw, Z_mask_row, ln1_w, ln1_b, lrp_w, lrp_b, gate_w, gate_b, og_w, og_b, ln2_w, ln2_b, op_w, out_bias):
        import jax, jax.numpy as jnp
        import numpy as np
        D_PAIR = 32
        C = 32
        LN_EPS = 1e-05

        def _layernorm(x, w, b):
            m = jnp.mean(x, axis=-1, keepdims=True)
            v = jnp.var(x, axis=-1, keepdims=True)
            return (x - m) * jax.lax.rsqrt(v + LN_EPS) * w + b
        z = _layernorm(Z_raw, ln1_w, ln1_b)
        g = jax.nn.sigmoid(z @ gate_w.T + gate_b)
        proj = (z @ lrp_w.T + lrp_b) * Z_mask_row[..., None] * g
        left, right = jnp.split(proj, 2, axis=-1)
        tri = jnp.einsum('bikc,bjkc->bijc', left, right)
        go = jax.nn.sigmoid(tri @ og_w.T + og_b)
        z2 = _layernorm(tri, ln2_w, ln2_b) @ op_w.T
        return tri + go * (z2 + out_bias)

    def _L0_ffn_ref(x, router_w, router_b, expert_w, expert_b):
        import jax, jax.numpy as jnp
        import numpy as np
        B, N, D, C, E, K = (8, 2048, 32, 32, 8, 2)
        router_probs = jax.nn.softmax(x @ router_w + router_b, axis=-1)
        top_p, top_i = jax.lax.top_k(router_probs, K)
        top_p = top_p / jnp.sum(top_p, axis=-1, keepdims=True)
        expert_out = jnp.einsum('bnd,edc->bnec', x, expert_w) + expert_b
        gathered = jnp.take_along_axis(expert_out, top_i[..., None], axis=2)
        return jnp.einsum('bnk,bnkc->bnc', top_p, gathered)

    def _gn(v, G=32, eps=1e-05):
        B_, H_, W_, C_ = v.shape
        g = v.reshape(B_, H_, W_, G, C_ // G)
        m = jnp.mean(g, axis=(1, 2, 4), keepdims=True)
        s = jnp.var(g, axis=(1, 2, 4), keepdims=True)
        return ((g - m) / jnp.sqrt(s + eps)).reshape(v.shape)

    def _ln_c(v, eps=1e-06):
        m = jnp.mean(v, axis=-1, keepdims=True)
        s = jnp.var(v, axis=-1, keepdims=True)
        return (v - m) / jnp.sqrt(s + eps)

    def _ln_t(v, eps=1e-05):
        m = jnp.mean(v, axis=-1, keepdims=True)
        s = jnp.var(v, axis=-1, keepdims=True)
        return (v - m) / jnp.sqrt(s + eps)

    def _to_tokens(v):
        B_, H_, W_, C_ = v.shape
        return v.reshape(B_, H_ * W_, C_)

    def _from_tokens(t, like):
        return t.reshape(like.shape)
    x = x + _L0_conv_ref(_ln_c(x), L0_conv_Z_mask_row, L0_conv_ln1_w, L0_conv_ln1_b, L0_conv_lrp_w, L0_conv_lrp_b, L0_conv_gate_w, L0_conv_gate_b, L0_conv_og_w, L0_conv_og_b, L0_conv_ln2_w, L0_conv_ln2_b, L0_conv_op_w, L0_conv_out_bias)
    t = _to_tokens(x)
    t = t + _L0_ffn_ref(_ln_t(t), L0_ffn_router_w, L0_ffn_router_b, L0_ffn_expert_w, L0_ffn_expert_b)
    x = _from_tokens(t, x)
    return x

_drawn_inputs = setup_inputs


def setup_inputs(seed=0):
    import zlib

    import numpy as np

    out = dict(_drawn_inputs(seed))
    spreads = {'L0_conv_Z_mask_row': (1.0, 0.2),
     'L0_conv_ln1_w': (1.0, 0.2),
     'L0_conv_ln1_b': (0.0, 0.1),
     'L0_conv_lrp_b': (0.0, 0.1),
     'L0_conv_gate_b': (1.0, 0.2),
     'L0_conv_og_b': (1.0, 0.6),
     'L0_conv_ln2_w': (1.0, 0.6),
     'L0_conv_ln2_b': (0.0, 2.0),
     'L0_conv_out_bias': (0.0, 0.592),
     'L0_ffn_router_b': (0.0, 0.1),
     'L0_ffn_expert_b': (0.0, 0.8)}
    factors = {'L0_conv_gate_w': 5.398, 'L0_conv_og_w': 22.866, 'L0_conv_op_w': 8.0}
    for name, (base, spread) in spreads.items():
        noise = np.random.default_rng([zlib.crc32(name.encode()), seed]).standard_normal(out[name].shape)
        drawn = base * np.exp(spread * noise) if base else spread * noise
        out[name] = jnp.asarray(drawn.astype(out[name].dtype))
    for name, factor in factors.items():
        out[name] = (out[name] * factor).astype(out[name].dtype)
    return out
```

```python
from contextlib import ExitStack

import concourse.bass as bass
from concourse import mybir

P = 128
N = 128
C = 32
E = 8
R = P // C
F1 = 4 * C
G = 8
JG = N // G
W = JG * C
CH = JG // R
PARTS = 3
KW = R * PARTS * E

LN_C_EPS = 1e-6
LN_EPS = 1e-5

ALU = mybir.AluOpType
ACT = mybir.ActivationFunctionType
F32 = mybir.dt.float32
BF16 = mybir.dt.bfloat16
AX_X = mybir.AxisListType.X

EARLY = [("w1", R * F1), ("b1", R * F1), ("ln1_w", 1), ("ln1_b", 1), ("part", PARTS), ("ident", P),
         ("mask", N)]
LATE = [("w4", R * 2 * C), ("router", R * E), ("expert", 2 * C), ("eb", P), ("ln2_w", 1), ("ln2_b", 1),
        ("og_b", R * C), ("out_b", C), ("router_b", E), ("centre", P), ("sel", 2 * R * P), ("prio", E)]


def columns(parts):
    at, out = 0, {}
    for name, width in parts:
        out[name] = (at, width)
        at += width
    return out, at


def bass_metaformer(nc, x_k, x_i, early, late, out):
    ecol, EW = columns(EARLY)
    lcol, LW = columns(LATE)

    with ExitStack() as ctx:
        def sb(name, width, dt=F32):
            return ctx.enter_context(nc.sbuf_tensor(name, [P, width], dt))

        def sem(name):
            return ctx.enter_context(nc.semaphore(name))

        def grid(ap, inner=C):
            return ap.rearrange("p (j c) -> p j c", c=inner)

        ps = ctx.enter_context(nc.psum_tensor("ps", [P, 8, 512], F32))

        xk = sb("xk", N * C)
        xi = sb("xi", N * C)
        lr = sb("lr", 2 * C * N)
        tri = sb("tri", N * C)
        triF = sb("triF", N * C)
        x1 = xk
        x1F = lr[:, 0:N * C]
        x1c = lr[:, N * C:2 * N * C]
        early_sb = sb("early_sb", EW)
        late_sb = sb("late_sb", LW)
        ering = sb("ering", 2 * W)
        fring = sb("fring", 2 * W)
        gates = sb("gates", 4 * W)
        sq = sb("sq", 2 * W)
        stats = sb("stats", 4 * N)
        nmean, ssum, std, rstd = (stats[:, n * N:(n + 1) * N] for n in range(4))
        ones_b = sb("ones_b", P, BF16)
        ones_f = sb("ones_f", P)
        lnb = sb("lnb", P)
        w1 = sb("w1m", R * F1)
        split_a = sb("split_a", R * F1)
        split_b = sb("split_b", R * F1)
        part_b = sb("part_b", R * F1, BF16)
        bias1 = sb("bias1", R * F1, BF16)
        bias4 = sb("bias4", R * C, BF16)
        w4 = sb("w4m", R * 2 * C)
        w4in = sb("w4in", R * 2 * C)
        cb = sb("cb", C)
        rcm = sb("rcm", R * (C + E))
        ebp = sb("ebp", PARTS * P, BF16)
        selb = sb("selb", 2 * R * P, BF16)
        logit = sb("logit", N * E)
        tk = [sb(f"tk{n}", N * E) for n in range(3)]
        pair = sb("pair", 4 * N)
        w3 = sb("w3", N * PARTS * E, BF16)
        w3F = sb("w3F", N * N // R, BF16)
        xrep = sb("xrep", R * W)

        def ecp(name):
            a, w = ecol[name]
            return early_sb[:, a:a + w]

        def lcp(name):
            a, w = lcol[name]
            return late_sb[:, a:a + w]

        ident = ecp("ident")
        mask = ecp("mask")
        centre = lcp("centre")

        s_early = sem("early_loaded")
        s_late = sem("late_loaded")
        s_xk = [sem(f"xk_loaded{n}") for n in range(4)]
        s_xi = sem("xi_loaded")
        s_ones = sem("ones_ready")
        s_dve = sem("dve_step")
        s_mean = sem("mean_ready")
        s_sum = sem("sum_ready")
        s_cent = sem("centred")
        s_sq = sem("squares_ready")
        s_var = sem("variance_ready")
        s_std = sem("std_ready")
        s_lnb = sem("shift_ready")
        s_brow = sem("bias_row_ready")
        s_w1 = sem("w1_ready")
        s_xs = sem("scaled_ready")
        s_tp = sem("transposed")
        s_xT = sem("xT_ready")
        s_proj = sem("projected")
        s_gate = sem("gate_ready")
        s_gm = sem("masked_gate_ready")
        s_lr = sem("lr_ready")
        s_tri = sem("tri_bank_ready")
        s_trs = sem("tri_stored")
        s_trd = sem("tri_stored_by_vector")
        s_res = sem("residual_ready")
        s_t4 = sem("tri_transposed")
        s_f4 = sem("triF_ready")
        s_c4 = sem("tri_centred")
        s_q4 = sem("tri_squares_ready")
        s_v4 = sem("tri_sums_ready")
        s_w4 = sem("w4_ready")
        s_go = sem("gate_and_update_ready")
        s_gs = sem("out_gate_ready")
        s_u1 = sem("update_scaled")
        s_u2 = sem("update_shifted")
        s_u3 = sem("update_gated")
        s_x1 = sem("x1_ready")
        s_t5 = sem("x1_transposed")
        s_f5 = sem("x1F_ready")
        s_c5 = sem("x1_centred")
        s_q5 = sem("x1_squares_ready")
        s_l5 = sem("logits_ready")
        s_v5 = sem("x1_sums_ready")
        s_w3 = sem("expert_weights_ready")
        s_wt = sem("weights_transposed")
        s_wf = sem("w3F_ready")
        s_xh = sem("xhat_ready")
        s_rep = sem("xhat_replicated")
        s_xr = sem("xrep_ready")
        s_wb = sem("weights_spread")
        s_pr = sem("products_ready")
        s_y = sem("experts_summed")
        s_yf = sem("result_F_ready")
        s_bk = sem("result_transposed")
        s_o = sem("result_T_ready")
        s_out = [sem(f"out_stored{n}") for n in range(2)]
        s_rstd = sem("rstd_ready")
        s_diff = sem("logit_difference_ready")
        s_prob = sem("probabilities_ready")

        block = ctx.enter_context(nc.Block())
        SPREAD = [2, 3, 6, 7]

        def prod(slot, n):
            return (tri, triF)[slot][:, n * W:(n + 1) * W]

        def xhat4(slot):
            return xi[:, slot * R * W:(slot + 1) * R * W]

        yF = sq
        ident_b = sb("ident_b", P, BF16)

        def wait(eng, semaphore, value):
            if not isinstance(value, int) or value > 0:
                eng.wait_ge(semaphore, value)

        def groups(eng, body):
            body(0, 0)
            body(1, 1)
            with eng.Fori(1, G // 2) as turn:
                body(turn * 2, 0)
                body(turn * 2 + 1, 1)

        def ahead(eng, first, then):
            first(0, 0)
            first(1, 1)
            then(0, 0)
            first(2, 0)
            then(1, 1)
            with eng.Fori(1, G // 2 - 1) as turn:
                first(turn * 2 + 1, 1)
                then(turn * 2, 0)
                first(turn * 2 + 2, 0)
                then(turn * 2 + 1, 1)
            first(G - 1, 1)
            then(G - 2, 0)
            then(G - 1, 1)

        def half(slot, p):
            b = 4 * slot + 2 * p
            return ps[:, b:b + 2, :].rearrange("p b (r f) -> p (b r) f", f=F1)

        @block.sync
        def _(sp):
            sp.dma_start(early_sb[:, :], early).then_inc(s_early, 16)
            QW = N * C // 4
            for n in range(4):
                sp.dma_start(xk[:, n * QW:(n + 1) * QW], x_k[:, n * QW:(n + 1) * QW]).then_inc(s_xk[n], 16)
            sp.dma_start(late_sb[:, :], late).then_inc(s_late, 16)
            sp.dma_start(xi[:, :], x_i).then_inc(s_xi, 16)

            def store(g, slot):
                sp.wait_ge(s_o, g + 1)
                sp.dma_start(out[:, bass.ds(g * W, W)], ering[:, slot * W:(slot + 1) * W])\
                    .then_inc(s_out[slot], 16)
            groups(sp, store)
            for stored in s_out:
                sp.wait_ge(stored, 16 * G // 2)

        @block.gpsimd
        def _(pool):
            pool.memset(ones_b[:, :], 1.0).then_inc(s_ones, 1)
            pool.memset(ones_f[:, :], 1.0).then_inc(s_ones, 1)
            QJ = N // 4

            for n in range(4):
                pool.wait_ge(s_mean, n + 1)
                v = grid(xk[:, n * QJ * C:(n + 1) * QJ * C])
                m = nmean[:, n * QJ:(n + 1) * QJ].unsqueeze(2).broadcast_to([P, QJ, C])
                pool.tensor_tensor(v, v, m, ALU.add).then_inc(s_cent, 1)

            def masked(g, slot):
                for p in range(2):
                    pool.wait_ge(s_gate, 2 * g + (p + 1))
                    v = grid(gates[:, (2 * slot + p) * W:(2 * slot + p + 1) * W], 2 * C)
                    m = mask[:, bass.ds(g * JG + 8 * p, 8)].unsqueeze(2).broadcast_to([P, 8, 2 * C])
                    pool.tensor_tensor(v, v, m, ALU.mult).then_inc(s_gm, 1)
            groups(pool, masked)

            pool.wait_ge(s_xi, 16)
            pool.wait_ge(s_trs, 4)
            pool.wait_ge(s_trd, 4)

            def residual(g, slot):
                pool.tensor_tensor(xi[:, bass.ds(g * W, W)], xi[:, bass.ds(g * W, W)],
                                   tri[:, bass.ds(g * W, W)], ALU.add).then_inc(s_res, 1)
            groups(pool, residual)

            def shifted(g, slot):
                pool.wait_ge(s_u1, g + 1)
                v = grid(sq[:, slot * W:(slot + 1) * W])
                pool.tensor_tensor(v, v, cb[:, :].unsqueeze(1).broadcast_to([P, JG, C]), ALU.add)\
                    .then_inc(s_u2, 1)
            groups(pool, shifted)

            pool.wait_ge(s_rstd, 1)

            def xhat(g, slot):
                wait(pool, s_rep, 4 * g - 4)
                pool.tensor_tensor(xhat4(slot).rearrange("p (j e c) -> p j e c", e=R, c=C),
                                   grid(x1c)[:, bass.ds(g * JG, JG), :].unsqueeze(2).broadcast_to([P, JG, R, C]),
                                   rstd[:, bass.ds(g * JG, JG)].unsqueeze(2).unsqueeze(3).broadcast_to([P, JG, R, C]),
                                   ALU.mult).then_inc(s_xh, 1)
            groups(pool, xhat)

        @block.scalar
        def _(act):
            def square_quarter(n):
                act.wait_ge(s_cent, n + 1)
                act.activation(gates_q(n), xk[:, n * 1024:(n + 1) * 1024], ACT.Square).then_inc(s_sq, 1)

            def gates_q(n):
                return gates[:, (n % 2) * 1024:(n % 2 + 1) * 1024]

            for n in range(4):
                if n >= 2:
                    act.wait_ge(s_sum, n - 1)
                square_quarter(n)
            act.wait_ge(s_var, 1)
            act.activation(std, ssum, ACT.Sqrt).then_inc(s_std, 1)

            def evacuate(g, slot):
                act.wait_ge(s_tp, g + 1)
                act.activation(fring[:, slot * W:(slot + 1) * W], ps[:, 4 * slot, :], ACT.Copy).then_inc(s_xT, 1)

            def gate(g, slot):
                for p in range(2):
                    act.wait_ge(s_proj, 2 * g + (p + 1))
                    act.activation(grid(gates[:, (2 * slot + p) * W:(2 * slot + p + 1) * W], 2 * C),
                                   half(slot, p)[:, :, 0:2 * C], ACT.Sigmoid).then_inc(s_gate, 1)

            ahead(act, evacuate, gate)

            for b in range(0, 8, 2):
                act.wait_ge(s_tri, b + 1)
                act.activation(grid(tri[:, :])[:, :, 4 * b:4 * b + 4].rearrange("p j c -> p c j"),
                               ps[:, b, :].rearrange("p (c j) -> p c j", c=4), ACT.Copy).then_inc(s_trs, 1)

            def triF_copy(g, slot):
                act.wait_ge(s_t4, g + 1)
                act.activation(triF[:, bass.ds(g * W, W)], ps[:, slot, :], ACT.Copy).then_inc(s_f4, 1)

            def square4(g, slot):
                act.wait_ge(s_c4, g + 1)
                wait(act, s_v4, g - 1)
                act.activation(gates[:, slot * W:(slot + 1) * W], ps[:, 2 + slot, :], ACT.Square).then_inc(s_q4, 1)

            ahead(act, triF_copy, square4)
            act.wait_ge(s_var, 2)
            act.activation(std, ssum, ACT.Sqrt).then_inc(s_std, 1)

            def out_gate(g, slot):
                act.wait_ge(s_go, g + 1)
                wait(act, s_u3, g - 1)
                act.activation(grid(gates[:, slot * W:(slot + 1) * W]),
                               grid(ps[:, 4 + 2 * slot, :]),
                               ACT.Sigmoid).then_inc(s_gs, 1)
            groups(act, out_gate)

            def x1F_copy(g, slot):
                act.wait_ge(s_t5, g + 1)
                act.activation(x1F[:, bass.ds(g * W, W)], ps[:, slot, :], ACT.Copy).then_inc(s_f5, 1)

            def rc(slot):
                return ps[:, 2 + 2 * slot:4 + 2 * slot, 0:2 * R * (C + E)].rearrange("p b (j f) -> p b j f", f=C + E)

            def square5(g, slot):
                act.wait_ge(s_c5, g + 1)
                act.activation(x1c[:, bass.ds(g * W, W)].rearrange("p (b j c) -> p b j c", b=2, c=C),
                               rc(slot)[:, :, :, 0:C], ACT.Copy).then_inc(s_l5, 1)
                act.activation(logit[:, bass.ds(g * JG * E, JG * E)].rearrange("p (b j c) -> p b j c", b=2, c=E),
                               rc(slot)[:, :, :, C:C + E], ACT.Copy).then_inc(s_l5, 1)
                wait(act, s_v5, g - 1)
                act.activation(gates[:, (2 + slot) * W:(3 + slot) * W].rearrange("p (b j c) -> p b j c", b=2, c=C),
                               rc(slot)[:, :, :, 0:C], ACT.Square).then_inc(s_q5, 1)

            ahead(act, x1F_copy, square5)
            act.wait_ge(s_var, 3)
            act.activation(std, ssum, ACT.Sqrt).then_inc(s_std, 1)
            act.wait_ge(s_diff, 1)
            act.activation(pair[:, 2 * N:3 * N], pair[:, 0:N], ACT.Sigmoid, scale=-1.0).then_inc(s_prob, 1)
            act.activation(pair[:, 3 * N:4 * N], pair[:, 0:N], ACT.Sigmoid).then_inc(s_prob, 1)

            def w3F_copy(g, slot):
                act.wait_ge(s_wt, g + 1)
                act.activation(w3F[0:KW, bass.ds(g * W, W)], ps[0:KW, slot, 0:W // 2].bitcast(BF16),
                               ACT.Copy).then_inc(s_wf, 1)
            groups(act, w3F_copy)

            def replicate(g, slot):
                for r in range(R):
                    act.wait_ge(s_rep, 4 * g + (r + 1))
                    wait(act, s_pr, 8 * g + (2 * r - 6))
                    act.activation(xrep[:, r * W:(r + 1) * W], ps[:, r % 2, :], ACT.Copy).then_inc(s_xr, 1)

            def result(g, slot, stored):
                act.wait_ge(s_bk, g + 1)
                wait(act, s_out[slot], 16 * stored)
                act.activation(ering[:, slot * W:(slot + 1) * W], ps[:, 4 + slot, :], ACT.Copy).then_inc(s_o, 1)

            replicate(0, 0)
            replicate(1, 1)
            replicate(2, 0)
            result(0, 0, 0)
            replicate(3, 1)
            result(1, 1, 0)
            with act.Fori(2, G // 2) as turn:
                for n in range(2):
                    replicate(turn * 2 + n, n)
                    result(turn * 2 + (n - 2), n, turn - 1)
            result(G - 2, 0, G // 2 - 1)
            result(G - 1, 1, G // 2 - 1)

        @block.tensor
        def _(pe):
            pe.wait_ge(s_lnb, 1)
            pe.matmul(ps[:, 7, :], lnb[:, :], ecp("w1"), start=True, stop=True).then_inc(s_brow, 1)
            pe.wait_ge(s_w1, 1)

            def turn_x(g, slot):
                pe.wait_ge(s_xs, g + 1)
                wait(pe, s_lr, 2 * g - 2)
                for q in range(CH):
                    t = pe.transpose(ps[:, 4 * slot, q * P:(q + 1) * P],
                                     ering[:, slot * W + q * P:slot * W + (q + 1) * P], ident)
                t.then_inc(s_tp, 1)

            def project(g, slot):
                pe.wait_ge(s_xT, g + 1)
                for q in range(CH):
                    pe.matmul(ps[:, 4 * slot + q, :], fring[:, slot * W + q * P:slot * W + (q + 1) * P], w1[:, :],
                              start=True, stop=False)
                    m = pe.matmul(ps[:, 4 * slot + q, :], ones_b[:, :], bias1[:, :], start=False, stop=True)
                    if q % 2:
                        m.then_inc(s_proj, 1)

            ahead(pe, turn_x, project)

            pe.wait_ge(s_lr, 2 * G)
            for c in range(C):
                m = pe.matmul(ps[:, c // 4, (c % 4) * N:(c % 4 + 1) * N], lr[:, c * N:(c + 1) * N],
                              lr[:, (C + c) * N:(C + c + 1) * N], start=True, stop=True)
                if c % 4 == 3:
                    m.then_inc(s_tri, 1)

            def turn_tri(g):
                for q in range(CH):
                    t = pe.transpose(ps[:, g % 2, q * P:(q + 1) * P], tri[:, g * W + q * P:g * W + (q + 1) * P], ident)
                t.then_inc(s_t4, 1)

            def centre_tri(g):
                pe.wait_ge(s_f4, g + 1)
                if g >= 2:
                    pe.wait_ge(s_q4, g - 1)
                for q in range(CH):
                    m = pe.matmul(ps[:, 2 + g % 2, q * P:(q + 1) * P], triF[:, g * W + q * P:g * W + (q + 1) * P],
                                  centre, start=True, stop=True)
                m.then_inc(s_c4, 1)

            pe.wait_ge(s_trs, 4)
            pe.wait_ge(s_trd, 4)
            turn_tri(0)
            for g in range(G):
                if g + 1 < G:
                    if g >= 1:
                        pe.wait_ge(s_f4, g)
                    turn_tri(g + 1)
                centre_tri(g)

            pe.wait_ge(s_lnb, 2)
            pe.matmul(ps[:, 4, 0:R * 2 * C], lnb[:, :], lcp("w4"), start=True, stop=True).then_inc(s_brow, 1)
            pe.matmul(ps[:, 5, 0:R * 2 * C], centre, w4in[:, :], start=True, stop=True).then_inc(s_brow, 1)
            pe.matmul(ps[:, 6, 0:R * E], centre, lcp("router"), start=True, stop=True).then_inc(s_brow, 1)
            pe.wait_ge(s_w4, 1)

            def gate_update(g):
                if g >= 2:
                    pe.wait_ge(s_gs, g - 1)
                    pe.wait_ge(s_u1, g - 1)
                for q in range(CH):
                    chunk = triF[:, g * W + q * P:g * W + (q + 1) * P]
                    cols = slice(q * P, (q + 1) * P)
                    pe.matmul(ps[:, 4 + 2 * (g % 2), cols], chunk, w4[:, 0:P], start=True, stop=False)
                    pe.matmul(ps[:, 4 + 2 * (g % 2), cols], ones_b[:, :], bias4[:, :], start=False, stop=True)
                    m = pe.matmul(ps[:, 5 + 2 * (g % 2), cols], chunk, w4[:, P:2 * P], start=True, stop=True)
                m.then_inc(s_go, 1)

            for g in range(G):
                gate_update(g)

            def turn_x1(g):
                pe.wait_ge(s_x1, g + 1)
                for q in range(CH):
                    t = pe.transpose(ps[:, g % 2, q * P:(q + 1) * P], x1[:, g * W + q * P:g * W + (q + 1) * P], ident)
                t.then_inc(s_t5, 1)

            def centre_x1(g):
                pe.wait_ge(s_f5, g + 1)
                if g >= 2:
                    pe.wait_ge(s_q5, g - 1)
                elif g == 0:
                    pe.wait_ge(s_u1, G)
                    pe.wait_ge(s_gs, G)
                    pe.wait_ge(s_q4, G)
                for q in range(CH):
                    m = pe.matmul(ps[:, 2 + 2 * (g % 2) + q // 2, (q % 2) * R * (C + E):(q % 2 + 1) * R * (C + E)],
                                  x1F[:, g * W + q * P:g * W + (q + 1) * P], rcm[:, :], start=True, stop=True)
                m.then_inc(s_c5, 1)

            turn_x1(0)
            for g in range(G):
                if g + 1 < G:
                    if g >= 1:
                        pe.wait_ge(s_f5, g)
                    turn_x1(g + 1)
                centre_x1(g)

            pe.wait_ge(s_w3, 1)
            for g in range(G):
                if g >= 2:
                    pe.wait_ge(s_wf, g - 1)
                for q in range(CH):
                    n = g * CH + q
                    t = pe.transpose(ps[0:KW, g % 2, q * P // 2:(q + 1) * P // 2].bitcast(BF16),
                                     w3[:, n * KW:(n + 1) * KW], ident_b[:, :])
                t.then_inc(s_wt, 1)
            pe.wait_ge(s_wf, G)
            pe.wait_ge(s_q5, G)

            def spread(g, slot):
                pe.wait_ge(s_xh, g + 1)
                for r in range(R):
                    wait(pe, s_xr, 4 * g + (r - 1))
                    for q in range(CH):
                        at = (q * R + r) * P
                        t = pe.transpose(ps[:, r % 2, q * P:(q + 1) * P],
                                         xhat4(slot)[:, at:at + P], ident)
                    t.then_inc(s_rep, 1)
                    for h in range(2):
                        n = 2 * r + h
                        wait(pe, s_pr, 8 * g + (n - 3))
                        pe.matmul(ps[:, SPREAD[n % 4], :], selb[0:KW, (r * 2 + h) * P:(r * 2 + h + 1) * P],
                                  w3F[0:KW, bass.ds(g * W, W)], start=True, stop=True).then_inc(s_wb, 1)

            def sum_experts(g, slot):
                wait(pe, s_o, g - 1)
                for n in range(PARTS):
                    pe.matmul(ps[:, 4 + slot, :], ebp[0:KW, n * P:(n + 1) * P], w3F[0:KW, bass.ds(g * W, W)],
                              start=(n == 0), stop=False, skip_group_check=True)
                pe.wait_ge(s_pr, 8 * g + 8)
                for h in range(2):
                    for r in range(R):
                        m = pe.matmul(ps[C * r:C * r + C, 4 + slot, :], lcp("expert")[:, h * C:(h + 1) * C],
                                      prod(slot, 2 * r + h), start=False, stop=(h == 1), skip_group_check=True)
                m.then_inc(s_y, 1)

            def turn_back(g, slot):
                pe.wait_ge(s_yf, g + 1)
                for q in range(CH):
                    t = pe.transpose(ps[:, 4 + slot, q * P:(q + 1) * P],
                                     yF[:, slot * W + q * P:slot * W + (q + 1) * P], ident)
                t.then_inc(s_bk, 1)

            spread(0, 0)
            spread(1, 1)
            sum_experts(0, 0)
            spread(2, 0)
            sum_experts(1, 1)
            turn_back(0, 0)
            spread(3, 1)
            sum_experts(2, 0)
            turn_back(1, 1)
            with pe.Fori(2, G // 2) as turn:
                for n in range(2):
                    spread(turn * 2 + n, n)
                    sum_experts(turn * 2 + (n - 1), 1 - n)
                    turn_back(turn * 2 + (n - 2), n)
            sum_experts(G - 1, 1)
            turn_back(G - 2, 0)
            turn_back(G - 1, 1)

        @block.vector
        def _(dve):
            steps = [0]

            def link(ins):
                steps[0] += 1
                ins.then_inc(s_dve, 1)
                dve.wait_ge(s_dve, steps[0])

            def over(small, n, inner):
                return small.unsqueeze(2).broadcast_to([P, n, inner])

            def split_selected(value, other, part, to):
                sel = ecp("part")
                link(dve.tensor_copy(part, value))
                link(dve.tensor_scalar(other, part, sel[:, 0:1], None, ALU.mult))
                link(dve.tensor_tensor(value, value, part, ALU.subtract))
                link(dve.tensor_copy(part, value))
                link(dve.scalar_tensor_tensor(out=other, in0=part, scalar=sel[:, 1:2], in1=other,
                                              op0=ALU.mult, op1=ALU.add))
                link(dve.tensor_tensor(value, value, part, ALU.subtract))
                link(dve.tensor_copy(part, value))
                link(dve.scalar_tensor_tensor(out=to, in0=part, scalar=sel[:, 2:3], in1=other,
                                              op0=ALU.mult, op1=ALU.add))

            dve.wait_ge(s_early, 16)
            dve.wait_ge(s_ones, 2)
            dve.tensor_scalar(lnb[:, :], ones_f[:, :], ecp("ln1_b"), None, ALU.mult).then_inc(s_lnb, 1)
            link(dve.tensor_scalar(w1[:, :], ecp("w1"), ecp("ln1_w"), None, ALU.mult))

            QJ = N // 4
            for n in range(4):
                dve.wait_ge(s_xk[n], 16)
                link(dve.tensor_reduce(ssum[:, n * QJ:(n + 1) * QJ], grid(xk[:, n * QJ * C:(n + 1) * QJ * C]),
                                       AX_X, ALU.add))
                dve.tensor_scalar(nmean[:, n * QJ:(n + 1) * QJ], ssum[:, n * QJ:(n + 1) * QJ], -1.0 / C, None,
                                  ALU.mult).then_inc(s_mean, 1)

            dve.wait_ge(s_brow, 1)
            link(dve.tensor_tensor(split_a[:, :], ps[:, 7, :], ecp("b1"), ALU.add))
            split_selected(split_a[:, :], split_b[:, :], part_b[:, :], bias1[:, :])
            dve.tensor_copy(ident_b[:, :], ident).then_inc(s_w1, 1)

            for n in range(4):
                dve.wait_ge(s_sq, n + 1)
                link(dve.tensor_reduce(ssum[:, n * QJ:(n + 1) * QJ],
                                       grid(gates[:, (n % 2) * 1024:(n % 2 + 1) * 1024]), AX_X, ALU.add))
                dve.engine_nop().then_inc(s_sum, 1)

            def normaliser(scale, shift, turn):
                dve.tensor_scalar(ssum, ssum, scale, shift, ALU.mult, ALU.add).then_inc(s_var, 1)
                dve.wait_ge(s_std, turn)
                link(dve.reciprocal(rstd, std))

            normaliser((1.0 + LN_EPS) / C, LN_C_EPS * LN_EPS, 1)

            def scaled(g, slot):
                wait(dve, s_tp, g - 1)
                dve.tensor_tensor(grid(ering[:, slot * W:(slot + 1) * W]), grid(xk[:, :])[:, bass.ds(g * JG, JG), :],
                                  over(rstd[:, bass.ds(g * JG, JG)], JG, C), ALU.mult).then_inc(s_xs, 1)

            def gated(g, slot):
                for p in range(2):
                    dve.wait_ge(s_gm, 2 * g + (p + 1))
                    dve.tensor_tensor(lr[:, :].rearrange("p (f i) -> p i f", i=N)[:, bass.ds(g * JG + 8 * p, 8), :],
                                      half(slot, p)[:, :, 2 * C:4 * C],
                                      grid(gates[:, (2 * slot + p) * W:(2 * slot + p + 1) * W], 2 * C),
                                      ALU.mult).then_inc(s_lr, 1)
            ahead(dve, scaled, gated)

            dve.wait_ge(s_late, 16)
            dve.tensor_scalar(w4in[:, :], lcp("w4"), lcp("ln2_w"), None, ALU.mult)
            link(dve.tensor_scalar(lnb[:, :], ones_f[:, :], lcp("ln2_b"), None, ALU.mult))
            dve.engine_nop().then_inc(s_lnb, 1)
            link(dve.tensor_copy(split_a[:, 0:R * C], lcp("og_b")))
            split_selected(split_a[:, 0:R * C], split_b[:, 0:R * C], part_b[:, 0:R * C], bias4[:, :])
            link(dve.tensor_copy(selb[:, :], lcp("sel")))
            link(dve.tensor_copy(ebp[:, 0:P], lcp("eb")))
            link(dve.tensor_tensor(split_a[:, 0:P], lcp("eb"), ebp[:, 0:P], ALU.subtract))
            link(dve.tensor_copy(ebp[:, P:2 * P], split_a[:, 0:P]))
            link(dve.tensor_tensor(split_a[:, 0:P], split_a[:, 0:P], ebp[:, P:2 * P], ALU.subtract))
            link(dve.tensor_copy(ebp[:, 2 * P:3 * P], split_a[:, 0:P]))

            for b in range(1, 8, 2):
                dve.wait_ge(s_tri, b + 1)
                dve.tensor_copy(grid(tri[:, :])[:, :, 4 * b:4 * b + 4].rearrange("p j c -> p c j"),
                                ps[:, b, :].rearrange("p (c j) -> p c j", c=4)).then_inc(s_trd, 1)

            def sums(squares, done, at):
                def body(g, slot):
                    dve.wait_ge(squares, g + 1)
                    dve.tensor_reduce(ssum[:, bass.ds(g * JG, JG)], grid(gates[:, (at + slot) * W:(at + slot + 1) * W]),
                                      AX_X, ALU.add).then_inc(done, 1)
                return body
            groups(dve, sums(s_q4, s_v4, 0))
            dve.wait_ge(s_v4, G)
            dve.tensor_scalar(ssum, ssum, 1.0 / C, LN_EPS, ALU.mult, ALU.add).then_inc(s_var, 1)

            dve.wait_ge(s_brow, 4)
            rv = rcm[:, :].rearrange("p (r f) -> p r f", f=C + E)
            link(dve.tensor_tensor(cb[:, :], ps[:, 4, P:P + C], lcp("out_b"), ALU.add))
            link(dve.tensor_copy(w4[:, 0:P], lcp("w4")[:, 0:P]))
            link(dve.tensor_copy(w4[:, P:2 * P], ps[:, 5, P:2 * P]))
            link(dve.tensor_copy(rv[:, :, 0:C], centre.rearrange("p (r c) -> p r c", c=C)))
            dve.tensor_copy(rv[:, :, C:C + E], ps[:, 6, 0:R * E].rearrange("p (r e) -> p r e", e=E)).then_inc(s_w4, 1)
            dve.wait_ge(s_std, 2)
            link(dve.reciprocal(rstd, std))

            def update(g, slot):
                dve.wait_ge(s_go, g + 1)
                wait(dve, s_x1, g - 1)
                dve.tensor_tensor(grid(sq[:, slot * W:(slot + 1) * W]),
                                  grid(ps[:, 5 + 2 * slot, :]),
                                  over(rstd[:, bass.ds(g * JG, JG)], JG, C), ALU.mult).then_inc(s_u1, 1)

            def close(g, slot):
                dve.wait_ge(s_u2, g + 1)
                dve.wait_ge(s_gs, g + 1)
                v = sq[:, slot * W:(slot + 1) * W]
                dve.tensor_tensor(v, v, gates[:, slot * W:(slot + 1) * W], ALU.mult).then_inc(s_u3, 1)
                dve.wait_ge(s_res, g + 1)
                dve.wait_ge(s_u3, g + 1)
                dve.tensor_tensor(x1[:, bass.ds(g * W, W)], v, xi[:, bass.ds(g * W, W)], ALU.add).then_inc(s_x1, 1)
            ahead(dve, update, close)

            groups(dve, sums(s_q5, s_v5, 2))
            dve.wait_ge(s_v5, G)
            normaliser(1.0 / C, LN_EPS, 3)
            dve.engine_nop().then_inc(s_rstd, 1)

            dve.wait_ge(s_l5, 2 * G)
            lg, first, rest, second = (grid(t[:, :], E) for t in (logit, *tk))
            prio = lcp("prio").unsqueeze(1).broadcast_to([P, N, E])
            best, gap = pair[:, N:2 * N], pair[:, 0:N]
            p1, p2 = pair[:, 2 * N:3 * N], pair[:, 3 * N:4 * N]
            top = ssum

            link(dve.tensor_tensor(lg, lg, over(rstd, N, E), ALU.mult))
            link(dve.tensor_tensor(lg, lg, lcp("router_b").unsqueeze(1).broadcast_to([P, N, E]), ALU.add))

            def one_hot(values, largest, to):
                link(dve.tensor_reduce(largest, values, AX_X, ALU.max))
                link(dve.tensor_tensor(to, values, over(largest, N, E), ALU.is_equal))
                link(dve.tensor_tensor(to, to, prio, ALU.mult))
                link(dve.tensor_reduce(top, to, AX_X, ALU.max))
                link(dve.tensor_tensor(to, to, over(top, N, E), ALU.is_equal))

            one_hot(lg, best, first)
            link(dve.scalar_tensor_tensor(out=tk[1][:, :], in0=tk[0][:, :], scalar=-1e30, in1=logit[:, :],
                                          op0=ALU.mult, op1=ALU.add))
            one_hot(rest, gap, second)
            link(dve.tensor_tensor(gap, gap, best, ALU.subtract))
            dve.engine_nop().then_inc(s_diff, 1)
            dve.wait_ge(s_prob, 2)
            link(dve.tensor_tensor(first, first, over(p1, N, E), ALU.mult))
            link(dve.tensor_tensor(second, second, over(p2, N, E), ALU.mult))
            link(dve.tensor_tensor(first, first, second, ALU.add))
            w3v = w3[:, :].rearrange("p (j n e) -> p j n e", n=PARTS, e=E)
            link(dve.tensor_copy(w3v[:, :, 0, :], first))
            link(dve.tensor_tensor(first, first, w3v[:, :, 0, :], ALU.subtract))
            link(dve.tensor_copy(w3v[:, :, 1, :], first))
            link(dve.tensor_tensor(first, first, w3v[:, :, 1, :], ALU.subtract))
            dve.tensor_copy(w3v[:, :, 2, :], first).then_inc(s_w3, 1)

            def products(g, slot):
                wait(dve, s_y, g - 1)
                for r in range(R):
                    dve.wait_ge(s_xr, 4 * g + (r + 1))
                    for h in range(2):
                        n = 2 * r + h
                        dve.wait_ge(s_wb, 8 * g + (n + 1))
                        dve.tensor_tensor(prod(slot, n), ps[:, SPREAD[n % 4], :], xrep[:, r * W:(r + 1) * W],
                                          ALU.mult).then_inc(s_pr, 1)

            def add_x1(g, slot):
                dve.wait_ge(s_y, g + 1)
                wait(dve, s_bk, g - 1)
                dve.tensor_tensor(yF[:, slot * W:(slot + 1) * W], ps[:, 4 + slot, :],
                                  x1F[:, bass.ds(g * W, W)], ALU.add).then_inc(s_yf, 1)
            ahead(dve, products, add_x1)


_OUT = ((1, N, N, C), "float32")


def kernel(**inputs):
    import numpy as _np
    import concourse.bacc as _bacc
    from concourse import mybir as _mybir
    from concourse.bass_utils import run_bass_kernel_spmd as _run

    a = {k.replace("L0_conv_", "").replace("L0_ffn_", ""): _np.asarray(v) for k, v in inputs.items()}
    f32 = a["x"].dtype

    def blocks(m):
        out = _np.zeros((R, m.shape[0], R, m.shape[1]), f32)
        for r in range(R):
            out[r, :, r, :] = m
        return out.reshape(R * m.shape[0], R * m.shape[1])

    def rows(v, times=1):
        return _np.tile(v, times)[None, :].repeat(P, axis=0)

    def column(v):
        return _np.tile(v, R)[:, None]

    ident = _np.eye(P, dtype=f32)
    centre = blocks(_np.eye(C, dtype=f32) - _np.full((C, C), 1.0 / C, f32))
    part = _np.eye(P, PARTS, dtype=f32)
    sel = _np.zeros((R, PARTS, E, R, 2, R, C), f32)
    for r in range(R):
        for e in range(E):
            sel[r, :, e, r, e // R, e % R, :] = 1.0
    sel = _np.concatenate([sel.reshape(KW, -1), _np.zeros((P - KW, 2 * R * P), f32)])
    prio = rows(_np.arange(E, 0, -1).astype(f32))

    eb = _np.zeros((R, PARTS, E, R, C), f32)
    for r in range(R):
        eb[r, :, :, r, :] = a["expert_b"][None]
    eb = _np.concatenate([eb.reshape(KW, P), _np.zeros((P - KW, P), f32)])
    fields = {
        "w1": blocks(_np.concatenate([a["gate_w"].T, a["lrp_w"].T], axis=1)),
        "b1": rows(_np.concatenate([a["gate_b"], a["lrp_b"]]), R),
        "ln1_w": column(a["ln1_w"]), "ln1_b": column(a["ln1_b"]), "part": part, "ident": ident,
        "mask": a["Z_mask_row"][0].T,
        "w4": _np.concatenate([blocks(a["og_w"].T), blocks(a["op_w"].T)], axis=1),
        "router": blocks(a["router_w"]),
        "expert": a["expert_w"].reshape(2, R * C, C).transpose(1, 0, 2).reshape(P, 2 * C),
        "eb": eb, "ln2_w": column(a["ln2_w"]), "ln2_b": column(a["ln2_b"]),
        "og_b": rows(a["og_b"], R), "out_b": rows(a["out_bias"]), "router_b": rows(a["router_b"]),
        "centre": centre, "sel": sel, "prio": prio,
    }
    x = a["x"][0]
    arrays = {
        "in_x_k": _np.ascontiguousarray(x.transpose(1, 0, 2)).reshape(N, N * C),
        "in_x_i": _np.ascontiguousarray(x).reshape(N, N * C),
        "in_early": _np.ascontiguousarray(_np.concatenate([fields[n] for n, _ in EARLY], axis=1)),
        "in_late": _np.ascontiguousarray(_np.concatenate([fields[n] for n, _ in LATE], axis=1)),
    }
    nc = _bacc.Bacc("TRN2", target_bir_lowering=False, num_devices=1)
    args = [nc.dram_tensor(n, v.shape, _mybir.dt.from_np(v.dtype), kind="ExternalInput").ap()
            for n, v in arrays.items()]
    out = nc.dram_tensor("out_0", (N, N * C), _mybir.dt.from_np(_np.dtype(_OUT[1])), kind="ExternalOutput").ap()
    bass_metaformer(nc, *args, out)
    r = _run(nc, [arrays], core_ids=[0])
    return r.results[0]["out_0"].reshape(_OUT[0])
```

```python
from contextlib import ExitStack

import concourse.bass as bass
from concourse import mybir

P = 128
N = 128
C = 32
E = 8
R = P // C
F1 = 4 * C
G = 8
JG = N // G
W = JG * C
CH = JG // R
PARTS = 3
KW = R * PARTS * E

LN_C_EPS = 1e-6
LN_EPS = 1e-5

ALU = mybir.AluOpType
ACT = mybir.ActivationFunctionType
F32 = mybir.dt.float32
BF16 = mybir.dt.bfloat16
AX_X = mybir.AxisListType.X

EARLY = [("w1", R * F1), ("b1", R * F1), ("ln1_w", 1), ("ln1_b", 1), ("centre", P), ("mean", P), ("ident", P),
         ("mask", N)]
LATE = [("w4", R * 2 * C), ("router", R * E), ("expert", 2 * C), ("expert_b", 2 * C), ("ln2_w", 1), ("ln2_b", 1),
        ("og_b", R * C), ("out_b", C), ("router_b", E), ("part", PARTS), ("sel", 2 * R * P), ("prio", E)]


def columns(parts):
    at, out = 0, {}
    for name, width in parts:
        out[name] = (at, width)
        at += width
    return out, at


def bass_metaformer(nc, x_k, x_i, early, late, out):
    ecol, EW = columns(EARLY)
    lcol, LW = columns(LATE)

    with ExitStack() as ctx:
        def sb(name, width, dt=F32):
            return ctx.enter_context(nc.sbuf_tensor(name, [P, width], dt))

        def sem(name):
            return ctx.enter_context(nc.semaphore(name))

        def grid(ap, inner=C):
            return ap.rearrange("p (j c) -> p j c", c=inner)

        ps = ctx.enter_context(nc.psum_tensor("ps", [P, 8, 512], F32))

        xk = sb("xk", N * C)
        xi = sb("xi", N * C)
        lr = sb("lr", 2 * C * N)
        tri = sb("tri", N * C)
        triF = sb("triF", N * C)
        x1 = xk
        x1F = lr[:, 0:N * C]
        x1c = lr[:, N * C:2 * N * C]
        early_sb = sb("early_sb", EW)
        late_sb = sb("late_sb", LW)
        ering = sb("ering", 2 * W)
        fring = sb("fring", 2 * W)
        gates = sb("gates", 4 * W)
        sq = sb("sq", 2 * W)
        stats = sb("stats", 4 * N)
        nmean, ssum, std, rstd = (stats[:, n * N:(n + 1) * N] for n in range(4))
        ones_b = sb("ones_b", P, BF16)
        ones_f = sb("ones_f", P)
        lnb = sb("lnb", P)
        w1in = sb("w1in", R * F1)
        wexp = sb("wexp", 2 * C)
        w1 = sb("w1m", R * F1)
        split_a = sb("split_a", R * C)
        split_b = sb("split_b", R * C)
        part_b = sb("part_b", R * C, BF16)
        bias4 = sb("bias4", R * C, BF16)
        w4 = sb("w4m", R * 2 * C)
        w4in = sb("w4in", R * 2 * C)
        cb = sb("cb", C)
        rcm = sb("rcm", R * (C + E))
        selb = sb("selb", 2 * R * P, BF16)
        logit = sb("logit", N * E)
        tk = [sb(f"tk{n}", N * E) for n in range(3)]
        pair = sb("pair", 4 * N)
        w3 = sb("w3", N * PARTS * E, BF16)
        w3F = sb("w3F", N * N // R, BF16)
        xrep = sb("xrep", R * W)

        def ecp(name):
            a, w = ecol[name]
            return early_sb[:, a:a + w]

        def lcp(name):
            a, w = lcol[name]
            return late_sb[:, a:a + w]

        ident = ecp("ident")
        mask = ecp("mask")
        centre = ecp("centre")

        s_early = sem("early_loaded")
        s_late = sem("late_loaded")
        s_xk = [sem(f"xk_loaded{n}") for n in range(4)]
        s_xi = sem("xi_loaded")
        s_ones = sem("ones_ready")
        s_dve = sem("dve_step")
        s_mean = sem("mean_ready")
        s_sum = sem("sum_ready")
        s_cent = sem("centred")
        s_sq = sem("squares_ready")
        s_var = sem("variance_ready")
        s_std = sem("std_ready")
        s_lnb = sem("shift_ready")
        s_brow = sem("bias_row_ready")
        s_w1 = sem("w1_ready")
        s_xs = sem("scaled_ready")
        s_tp = sem("transposed")
        s_xT = sem("xT_ready")
        s_proj = sem("projected")
        s_gate = sem("gate_ready")
        s_gm = sem("masked_gate_ready")
        s_lr = sem("lr_ready")
        s_tri = sem("tri_bank_ready")
        s_trs = sem("tri_stored")
        s_trd = sem("tri_stored_by_vector")
        s_res = sem("residual_ready")
        s_t4 = sem("tri_transposed")
        s_f4 = sem("triF_ready")
        s_c4 = sem("tri_centred")
        s_q4 = sem("tri_squares_ready")
        s_v4 = sem("tri_sums_ready")
        s_w4 = sem("w4_ready")
        s_go = sem("gate_and_update_ready")
        s_gs = sem("out_gate_ready")
        s_u1 = sem("update_scaled")
        s_u2 = sem("update_shifted")
        s_u3 = sem("update_gated")
        s_x1 = sem("x1_ready")
        s_t5 = sem("x1_transposed")
        s_f5 = sem("x1F_ready")
        s_c5 = sem("x1_centred")
        s_q5 = sem("x1_squares_ready")
        s_l5 = sem("logits_ready")
        s_v5 = sem("x1_sums_ready")
        s_norm = sem("logits_scaled")
        s_logit = sem("router_logits_ready")
        s_cand = sem("candidates_marked")
        s_rank = sem("candidates_ranked")
        s_rem = sem("remainder_ready")
        s_part = sem("part_ready")
        s_wt = sem("weights_transposed")
        s_wf = sem("w3F_ready")
        s_xh = sem("xhat_ready")
        s_rep = sem("xhat_replicated")
        s_xr = sem("xrep_ready")
        s_wb = sem("weights_spread")
        s_pr = sem("products_ready")
        s_y = sem("experts_summed")
        s_yf = sem("result_F_ready")
        s_bk = sem("result_transposed")
        s_o = sem("result_T_ready")
        s_out = [sem(f"out_stored{n}") for n in range(2)]
        s_rstd = sem("rstd_ready")
        s_diff = sem("logit_difference_ready")
        s_prob = sem("probabilities_ready")

        block = ctx.enter_context(nc.Block())
        SPREAD = [2, 3, 6, 7]

        def prod(slot, n):
            return (tri, triF)[slot][:, n * W:(n + 1) * W]

        def xhat4(slot):
            return xi[:, slot * R * W:(slot + 1) * R * W]

        def w3part(n, part):
            return w3[:, :].rearrange("p (h j n e) -> p h j n e", h=2, n=PARTS, e=E)[:, n, :, part, :]

        yF = sq
        ident_b = sb("ident_b", P, BF16)

        def wait(eng, semaphore, value):
            if not isinstance(value, int) or value > 0:
                eng.wait_ge(semaphore, value)

        def groups(eng, body):
            body(0, 0)
            body(1, 1)
            with eng.Fori(1, G // 2) as turn:
                body(turn * 2, 0)
                body(turn * 2 + 1, 1)

        def ahead(eng, first, then):
            first(0, 0)
            first(1, 1)
            then(0, 0)
            first(2, 0)
            then(1, 1)
            with eng.Fori(1, G // 2 - 1) as turn:
                first(turn * 2 + 1, 1)
                then(turn * 2, 0)
                first(turn * 2 + 2, 0)
                then(turn * 2 + 1, 1)
            first(G - 1, 1)
            then(G - 2, 0)
            then(G - 1, 1)

        def far_ahead(eng, first, then):
            first(0, 0)
            first(1, 1)
            for g in range(2):
                first(g + 2, g)
                then(g, g)
            with eng.Fori(1, G // 2 - 1) as turn:
                for n in range(2):
                    first(turn * 2 + (n + 2), n)
                    then(turn * 2 + n, n)
            then(G - 2, 0)
            then(G - 1, 1)

        def between(eng, before, first, after):
            first(0, 0)
            before(0, 0)
            first(1, 1)
            after(0, 0)
            before(1, 1)
            first(2, 0)
            after(1, 1)
            with eng.Fori(1, G // 2 - 1) as turn:
                for n in range(2):
                    before(turn * 2 + n, n)
                    first(turn * 2 + (n + 1), 1 - n)
                    after(turn * 2 + n, n)
            before(G - 2, 0)
            first(G - 1, 1)
            after(G - 2, 0)
            before(G - 1, 1)
            after(G - 1, 1)

        def half(slot, p):
            b = 4 * slot + 2 * p
            return ps[:, b:b + 2, :].rearrange("p b (r f) -> p (b r) f", f=F1)

        @block.sync
        def _(sp):
            sp.dma_start(early_sb[:, :], early).then_inc(s_early, 16)
            QW = N * C // 4
            for n in range(4):
                sp.dma_start(xk[:, n * QW:(n + 1) * QW], x_k[:, n * QW:(n + 1) * QW]).then_inc(s_xk[n], 16)
            sp.dma_start(late_sb[:, :], late).then_inc(s_late, 16)
            sp.dma_start(xi[:, :], x_i).then_inc(s_xi, 16)

            def store(g, slot):
                sp.wait_ge(s_o, g + 1)
                sp.dma_start(out[:, bass.ds(g * W, W)], ering[:, slot * W:(slot + 1) * W])\
                    .then_inc(s_out[slot], 16)
            groups(sp, store)
            for stored in s_out:
                sp.wait_ge(stored, 16 * G // 2)

        @block.gpsimd
        def _(pool):
            pool.memset(ones_b[:, :], 1.0).then_inc(s_ones, 1)
            pool.memset(ones_f[:, :], 1.0).then_inc(s_ones, 1)
            QJ = N // 4

            for n in range(4):
                pool.wait_ge(s_mean, n + 1)
                v = grid(xk[:, n * QJ * C:(n + 1) * QJ * C])
                m = nmean[:, n * QJ:(n + 1) * QJ].unsqueeze(2).broadcast_to([P, QJ, C])
                pool.tensor_tensor(v, v, m, ALU.add).then_inc(s_cent, 1)

            def masked(g, slot):
                for p in range(2):
                    pool.wait_ge(s_gate, 2 * g + (p + 1))
                    v = grid(gates[:, (2 * slot + p) * W:(2 * slot + p + 1) * W], 2 * C)
                    m = mask[:, bass.ds(g * JG + 8 * p, 8)].unsqueeze(2).broadcast_to([P, 8, 2 * C])
                    pool.tensor_tensor(v, v, m, ALU.mult).then_inc(s_gm, 1)
            groups(pool, masked)

            pool.wait_ge(s_xi, 16)
            pool.wait_ge(s_trs, 4)
            pool.wait_ge(s_trd, 4)

            def residual(g, slot):
                pool.tensor_tensor(xi[:, bass.ds(g * W, W)], xi[:, bass.ds(g * W, W)],
                                   tri[:, bass.ds(g * W, W)], ALU.add).then_inc(s_res, 1)
            groups(pool, residual)

            HE = N * E // 2

            def shifted(g, slot):
                pool.wait_ge(s_u1, g + 1)
                v = grid(sq[:, slot * W:(slot + 1) * W])
                pool.tensor_tensor(v, v, cb[:, :].unsqueeze(1).broadcast_to([P, JG, C]), ALU.add)\
                    .then_inc(s_u2, 1)
            groups(pool, shifted)

            pool.wait_ge(s_rstd, 1)
            pool.wait_ge(s_l5, 2 * G)
            for n in range(2):
                v = grid(logit[:, n * HE:(n + 1) * HE], E)
                pool.tensor_tensor(v, v, rstd[:, n * N // 2:(n + 1) * N // 2].unsqueeze(2)
                                   .broadcast_to([P, N // 2, E]), ALU.mult).then_inc(s_norm, 1)
            for n in range(2):
                v = grid(logit[:, n * HE:(n + 1) * HE], E)
                pool.wait_ge(s_norm, n + 1)
                pool.tensor_tensor(v, v, lcp("router_b").unsqueeze(1).broadcast_to([P, N // 2, E]),
                                   ALU.add).then_inc(s_logit, 1)
            for at in (0, 2):
                for n in range(2):
                    v = grid(tk[at][:, n * HE:(n + 1) * HE], E)
                    pool.wait_ge(s_cand, at + n + 1)
                    pool.tensor_tensor(v, v, lcp("prio").unsqueeze(1).broadcast_to([P, N // 2, E]),
                                       ALU.mult).then_inc(s_rank, 1)

            def xhat(g, slot):
                wait(pool, s_rep, 4 * g - 4)
                pool.tensor_tensor(xhat4(slot).rearrange("p (j e c) -> p j e c", e=R, c=C),
                                   grid(x1c)[:, bass.ds(g * JG, JG), :].unsqueeze(2).broadcast_to([P, JG, R, C]),
                                   rstd[:, bass.ds(g * JG, JG)].unsqueeze(2).unsqueeze(3).broadcast_to([P, JG, R, C]),
                                   ALU.mult).then_inc(s_xh, 1)
            groups(pool, xhat)

        @block.scalar
        def _(act):
            def square_quarter(n):
                act.wait_ge(s_cent, n + 1)
                act.activation(gates_q(n), xk[:, n * 1024:(n + 1) * 1024], ACT.Square).then_inc(s_sq, 1)

            def gates_q(n):
                return gates[:, (n % 2) * 1024:(n % 2 + 1) * 1024]

            for n in range(4):
                if n >= 2:
                    act.wait_ge(s_sum, n - 1)
                square_quarter(n)
            act.wait_ge(s_var, 1)
            act.activation(std, ssum, ACT.Sqrt).then_inc(s_std, 1)

            def evacuate(g, slot):
                act.wait_ge(s_tp, g + 1)
                act.activation(fring[:, slot * W:(slot + 1) * W], ps[:, 4 * slot, :], ACT.Copy, bias=1.0).then_inc(s_xT, 1)

            def gate(p):
                def body(g, slot):
                    act.wait_ge(s_proj, 2 * g + (p + 1))
                    act.activation(grid(gates[:, (2 * slot + p) * W:(2 * slot + p + 1) * W], 2 * C),
                                   half(slot, p)[:, :, 0:2 * C], ACT.Sigmoid).then_inc(s_gate, 1)
                return body

            between(act, gate(0), evacuate, gate(1))

            for b in range(0, 8, 2):
                act.wait_ge(s_tri, b + 1)
                act.activation(grid(tri[:, :])[:, :, 4 * b:4 * b + 4].rearrange("p j c -> p c j"),
                               ps[:, b, :].rearrange("p (c j) -> p c j", c=4), ACT.Copy).then_inc(s_trs, 1)

            def triF_copy(g, slot):
                act.wait_ge(s_t4, g + 1)
                act.activation(triF[:, bass.ds(g * W, W)], ps[:, slot, :], ACT.Copy).then_inc(s_f4, 1)

            def square4(g, slot):
                act.wait_ge(s_c4, g + 1)
                wait(act, s_v4, g - 1)
                act.activation(gates[:, slot * W:(slot + 1) * W], ps[:, 2 + slot, :], ACT.Square).then_inc(s_q4, 1)

            ahead(act, triF_copy, square4)
            act.wait_ge(s_var, 2)
            act.activation(std, ssum, ACT.Sqrt).then_inc(s_std, 1)

            def out_gate(g, slot):
                act.wait_ge(s_go, g + 1)
                wait(act, s_u3, g - 1)
                act.activation(grid(gates[:, slot * W:(slot + 1) * W]),
                               grid(ps[:, 4 + 2 * slot, :]),
                               ACT.Sigmoid).then_inc(s_gs, 1)
            groups(act, out_gate)

            def x1F_copy(g, slot):
                act.wait_ge(s_t5, g + 1)
                act.activation(x1F[:, bass.ds(g * W, W)], ps[:, slot, :], ACT.Copy).then_inc(s_f5, 1)

            def rc(slot):
                return ps[:, 2 + 2 * slot:4 + 2 * slot, 0:2 * R * (C + E)].rearrange("p b (j f) -> p b j f", f=C + E)

            def square5(g, slot):
                act.wait_ge(s_c5, g + 1)
                act.activation(x1c[:, bass.ds(g * W, W)].rearrange("p (b j c) -> p b j c", b=2, c=C),
                               rc(slot)[:, :, :, 0:C], ACT.Copy).then_inc(s_l5, 1)
                act.activation(logit[:, bass.ds(g * JG * E, JG * E)].rearrange("p (b j c) -> p b j c", b=2, c=E),
                               rc(slot)[:, :, :, C:C + E], ACT.Copy).then_inc(s_l5, 1)
                wait(act, s_v5, g - 1)
                act.activation(gates[:, (2 + slot) * W:(3 + slot) * W].rearrange("p (b j c) -> p b j c", b=2, c=C),
                               rc(slot)[:, :, :, 0:C], ACT.Square).then_inc(s_q5, 1)

            ahead(act, x1F_copy, square5)
            act.wait_ge(s_var, 3)
            act.activation(std, ssum, ACT.Sqrt).then_inc(s_std, 1)
            for n in range(2):
                lo, hi = n * N // 2, (n + 1) * N // 2
                act.wait_ge(s_diff, n + 1)
                act.activation(pair[:, 2 * N + lo:2 * N + hi], pair[:, N + lo:N + hi], ACT.Sigmoid,
                               scale=-1.0).then_inc(s_prob, 1)
                act.activation(pair[:, 3 * N + lo:3 * N + hi], pair[:, N + lo:N + hi], ACT.Sigmoid).then_inc(s_prob, 1)
            for part in range(PARTS):
                for n in range(2):
                    act.wait_ge(s_rem, 2 * part + n + 1)
                    act.activation(w3part(n, part), grid(tk[0][:, n * N * E // 2:(n + 1) * N * E // 2], E),
                                   ACT.Copy).then_inc(s_part, 1)

            def w3F_copy(g, slot):
                act.wait_ge(s_wt, g + 1)
                act.activation(w3F[0:KW, bass.ds(g * W, W)], ps[0:KW, slot, 0:W // 2].bitcast(BF16),
                               ACT.Copy).then_inc(s_wf, 1)
            groups(act, w3F_copy)

            def replicate(g, slot):
                for r in range(R):
                    act.wait_ge(s_rep, 4 * g + (r + 1))
                    wait(act, s_pr, 8 * g + (2 * r - 6))
                    act.activation(xrep[:, r * W:(r + 1) * W], ps[:, r % 2, :], ACT.Copy, bias=1.0).then_inc(s_xr, 1)

            def result(g, slot, stored):
                act.wait_ge(s_bk, g + 1)
                wait(act, s_out[slot], 16 * stored)
                act.activation(ering[:, slot * W:(slot + 1) * W], ps[:, 4 + slot, :], ACT.Copy).then_inc(s_o, 1)

            replicate(0, 0)
            replicate(1, 1)
            replicate(2, 0)
            result(0, 0, 0)
            replicate(3, 1)
            result(1, 1, 0)
            with act.Fori(2, G // 2) as turn:
                for n in range(2):
                    replicate(turn * 2 + n, n)
                    result(turn * 2 + (n - 2), n, turn - 1)
            result(G - 2, 0, G // 2 - 1)
            result(G - 1, 1, G // 2 - 1)

        @block.tensor
        def _(pe):
            pe.wait_ge(s_lnb, 1)
            pe.matmul(ps[:, 7, :], lnb[:, :], ecp("w1"), start=True, stop=False)
            pe.matmul(ps[:, 7, :], centre, w1in[:, :], start=False, stop=True).then_inc(s_brow, 1)

            pe.wait_ge(s_w1, 1)

            def turn_x(g, slot):
                pe.wait_ge(s_xs, g + 1)
                wait(pe, s_lr, 2 * g - 3)
                for q in range(CH):
                    t = pe.transpose(ps[:, 4 * slot, q * P:(q + 1) * P],
                                     ering[:, slot * W + q * P:slot * W + (q + 1) * P], ident)
                t.then_inc(s_tp, 1)

            def project(p):
                def body(g, slot):
                    if p == 0:
                        pe.wait_ge(s_xT, g + 1)
                    else:
                        wait(pe, s_lr, 2 * g - 2)
                    for q in range(2 * p, 2 * p + 2):
                        m = pe.matmul(ps[:, 4 * slot + q, :], fring[:, slot * W + q * P:slot * W + (q + 1) * P],
                                      w1[:, :], start=True, stop=True)
                    m.then_inc(s_proj, 1)
                return body

            between(pe, project(0), turn_x, project(1))

            pe.wait_ge(s_lr, 2 * G)
            for c in range(C):
                m = pe.matmul(ps[:, c // 4, (c % 4) * N:(c % 4 + 1) * N], lr[:, c * N:(c + 1) * N],
                              lr[:, (C + c) * N:(C + c + 1) * N], start=True, stop=True)
                if c % 4 == 3:
                    m.then_inc(s_tri, 1)

            def turn_tri(g):
                for q in range(CH):
                    t = pe.transpose(ps[:, g % 2, q * P:(q + 1) * P], tri[:, g * W + q * P:g * W + (q + 1) * P], ident)
                t.then_inc(s_t4, 1)

            def centre_tri(g):
                pe.wait_ge(s_f4, g + 1)
                if g >= 2:
                    pe.wait_ge(s_q4, g - 1)
                for q in range(CH):
                    m = pe.matmul(ps[:, 2 + g % 2, q * P:(q + 1) * P], triF[:, g * W + q * P:g * W + (q + 1) * P],
                                  centre, start=True, stop=True)
                m.then_inc(s_c4, 1)

            pe.wait_ge(s_trs, 4)
            pe.wait_ge(s_trd, 4)
            turn_tri(0)
            for g in range(G):
                if g + 1 < G:
                    if g >= 1:
                        pe.wait_ge(s_f4, g)
                    turn_tri(g + 1)
                centre_tri(g)

            pe.wait_ge(s_lnb, 2)
            pe.matmul(ps[:, 4, 0:R * 2 * C], lnb[:, :], lcp("w4"), start=True, stop=True).then_inc(s_brow, 1)
            pe.matmul(ps[:, 5, 0:R * 2 * C], centre, w4in[:, :], start=True, stop=True).then_inc(s_brow, 1)
            pe.matmul(ps[:, 6, 0:R * E], centre, lcp("router"), start=True, stop=True).then_inc(s_brow, 1)
            pe.matmul(ps[:, 7, 0:2 * C], centre, lcp("expert"), start=True, stop=True).then_inc(s_brow, 1)
            pe.wait_ge(s_w4, 1)

            def gate_update(g):
                if g >= 2:
                    pe.wait_ge(s_gs, g - 1)
                    pe.wait_ge(s_u1, g - 1)
                for q in range(CH):
                    chunk = triF[:, g * W + q * P:g * W + (q + 1) * P]
                    cols = slice(q * P, (q + 1) * P)
                    pe.matmul(ps[:, 4 + 2 * (g % 2), cols], chunk, w4[:, 0:P], start=True, stop=False)
                    pe.matmul(ps[:, 4 + 2 * (g % 2), cols], ones_b[:, :], bias4[:, :], start=False, stop=True)
                    m = pe.matmul(ps[:, 5 + 2 * (g % 2), cols], chunk, w4[:, P:2 * P], start=True, stop=True)
                m.then_inc(s_go, 1)

            for g in range(G):
                gate_update(g)

            def turn_x1(g):
                pe.wait_ge(s_x1, g + 1)
                for q in range(CH):
                    t = pe.transpose(ps[:, g % 2, q * P:(q + 1) * P], x1[:, g * W + q * P:g * W + (q + 1) * P], ident)
                t.then_inc(s_t5, 1)

            def centre_x1(g):
                pe.wait_ge(s_f5, g + 1)
                if g >= 2:
                    pe.wait_ge(s_q5, g - 1)
                elif g == 0:
                    pe.wait_ge(s_u1, G)
                    pe.wait_ge(s_gs, G)
                    pe.wait_ge(s_q4, G)
                for q in range(CH):
                    m = pe.matmul(ps[:, 2 + 2 * (g % 2) + q // 2, (q % 2) * R * (C + E):(q % 2 + 1) * R * (C + E)],
                                  x1F[:, g * W + q * P:g * W + (q + 1) * P], rcm[:, :], start=True, stop=True)
                m.then_inc(s_c5, 1)

            turn_x1(0)
            for g in range(G):
                if g + 1 < G:
                    if g >= 1:
                        pe.wait_ge(s_f5, g)
                    turn_x1(g + 1)
                centre_x1(g)

            pe.wait_ge(s_part, 2 * PARTS)
            for g in range(G):
                if g >= 2:
                    pe.wait_ge(s_wf, g - 1)
                for q in range(CH):
                    n = g * CH + q
                    t = pe.transpose(ps[0:KW, g % 2, q * P // 2:(q + 1) * P // 2].bitcast(BF16),
                                     w3[:, n * KW:(n + 1) * KW], ident_b[:, :])
                t.then_inc(s_wt, 1)
            pe.wait_ge(s_wf, G)
            pe.wait_ge(s_q5, G)

            def spread(g, slot, r):
                if r == 0:
                    pe.wait_ge(s_xh, g + 1)
                wait(pe, s_xr, 4 * g + (r - 1))
                for q in range(CH):
                    at = (q * R + r) * P
                    t = pe.transpose(ps[:, r % 2, q * P:(q + 1) * P], xhat4(slot)[:, at:at + P], ident)
                t.then_inc(s_rep, 1)
                for h in range(2):
                    n = 2 * r + h
                    wait(pe, s_pr, 8 * g + (n - 3))
                    pe.matmul(ps[:, SPREAD[n % 4], :], selb[0:KW, (r * 2 + h) * P:(r * 2 + h + 1) * P],
                              w3F[0:KW, bass.ds(g * W, W)], start=True, stop=True).then_inc(s_wb, 1)

            def sum_experts(g, slot, h):
                if h == 0:
                    wait(pe, s_o, g - 1)
                    pe.wait_ge(s_pr, 8 * g + 8)
                for r in range(R):
                    m = pe.matmul(ps[C * r:C * r + C, 4 + slot, :], wexp[:, h * C:(h + 1) * C],
                                  prod(slot, 2 * r + h), start=(h == 0), stop=(h == 1))
                if h == 1:
                    m.then_inc(s_y, 1)

            def turn_back(g, slot):
                pe.wait_ge(s_yf, g + 1)
                for q in range(CH):
                    t = pe.transpose(ps[:, 4 + slot, q * P:(q + 1) * P],
                                     yF[:, slot * W + q * P:slot * W + (q + 1) * P], ident)
                t.then_inc(s_bk, 1)

            def step(g, slot, sums, backs):
                spread(g, slot, 0)
                spread(g, slot, 1)
                if sums:
                    sum_experts(g - 1, 1 - slot, 0)
                spread(g, slot, 2)
                if sums:
                    sum_experts(g - 1, 1 - slot, 1)
                spread(g, slot, 3)
                if backs:
                    turn_back(g - 2, slot)

            step(0, 0, False, False)
            step(1, 1, True, False)
            step(2, 0, True, True)
            step(3, 1, True, True)
            with pe.Fori(2, G // 2) as turn:
                for n in range(2):
                    step(turn * 2 + n, n, True, True)
            turn_back(G - 2, 0)
            sum_experts(G - 1, 1, 0)
            sum_experts(G - 1, 1, 1)
            turn_back(G - 1, 1)

        @block.vector
        def _(dve):
            steps = [0]

            def link(ins):
                steps[0] += 1
                ins.then_inc(s_dve, 1)
                dve.wait_ge(s_dve, steps[0])

            def over(small, n, inner):
                return small.unsqueeze(2).broadcast_to([P, n, inner])

            def split_selected(value, other, part, to):
                sel = lcp("part")
                link(dve.tensor_copy(part, value))
                link(dve.tensor_scalar(other, part, sel[:, 0:1], None, ALU.mult))
                link(dve.tensor_tensor(value, value, part, ALU.subtract))
                link(dve.tensor_copy(part, value))
                link(dve.scalar_tensor_tensor(out=other, in0=part, scalar=sel[:, 1:2], in1=other,
                                              op0=ALU.mult, op1=ALU.add))
                link(dve.tensor_tensor(value, value, part, ALU.subtract))
                link(dve.tensor_copy(part, value))
                link(dve.scalar_tensor_tensor(out=to, in0=part, scalar=sel[:, 2:3], in1=other,
                                              op0=ALU.mult, op1=ALU.add))

            dve.wait_ge(s_early, 16)
            dve.wait_ge(s_ones, 2)
            link(dve.tensor_scalar(w1in[:, :], ecp("w1"), ecp("ln1_w"), None, ALU.mult))
            dve.tensor_scalar(lnb[:, :], ecp("mean"), ecp("ln1_b"), None, ALU.mult).then_inc(s_lnb, 1)

            QJ = N // 4
            for n in range(4):
                dve.wait_ge(s_xk[n], 16)
                link(dve.tensor_reduce(ssum[:, n * QJ:(n + 1) * QJ], grid(xk[:, n * QJ * C:(n + 1) * QJ * C]),
                                       AX_X, ALU.add))
                dve.tensor_scalar(nmean[:, n * QJ:(n + 1) * QJ], ssum[:, n * QJ:(n + 1) * QJ], -1.0 / C, None,
                                  ALU.mult).then_inc(s_mean, 1)

            dve.wait_ge(s_brow, 1)
            dve.scalar_tensor_tensor(out=w1[:, :], in0=ecp("b1"), scalar=1.0 / C, in1=ps[:, 7, :],
                                     op0=ALU.mult, op1=ALU.add).then_inc(s_w1, 1)

            for n in range(4):
                dve.wait_ge(s_sq, n + 1)
                link(dve.tensor_reduce(ssum[:, n * QJ:(n + 1) * QJ],
                                       grid(gates[:, (n % 2) * 1024:(n % 2 + 1) * 1024]), AX_X, ALU.add))
                dve.engine_nop().then_inc(s_sum, 1)

            def normaliser(scale, shift, turn):
                dve.tensor_scalar(ssum, ssum, scale, shift, ALU.mult, ALU.add).then_inc(s_var, 1)
                dve.wait_ge(s_std, turn)
                link(dve.reciprocal(rstd, std))

            normaliser((1.0 + LN_EPS) / C, LN_C_EPS * LN_EPS, 1)

            def scaled(g, slot):
                wait(dve, s_tp, g - 1)
                dve.tensor_tensor(grid(ering[:, slot * W:(slot + 1) * W]), grid(xk[:, :])[:, bass.ds(g * JG, JG), :],
                                  over(rstd[:, bass.ds(g * JG, JG)], JG, C), ALU.mult).then_inc(s_xs, 1)

            def gated(g, slot):
                for p in range(2):
                    dve.wait_ge(s_gm, 2 * g + (p + 1))
                    dve.tensor_tensor(lr[:, :].rearrange("p (f i) -> p i f", i=N)[:, bass.ds(g * JG + 8 * p, 8), :],
                                      half(slot, p)[:, :, 2 * C:4 * C],
                                      grid(gates[:, (2 * slot + p) * W:(2 * slot + p + 1) * W], 2 * C),
                                      ALU.mult).then_inc(s_lr, 1)
            far_ahead(dve, scaled, gated)

            dve.wait_ge(s_late, 16)
            dve.tensor_scalar(w4in[:, :], lcp("w4"), lcp("ln2_w"), None, ALU.mult)
            link(dve.tensor_scalar(lnb[:, :], ones_f[:, :], lcp("ln2_b"), None, ALU.mult))
            dve.engine_nop().then_inc(s_lnb, 1)
            link(dve.tensor_copy(split_a[:, 0:R * C], lcp("og_b")))
            split_selected(split_a[:, 0:R * C], split_b[:, 0:R * C], part_b[:, 0:R * C], bias4[:, :])
            link(dve.tensor_copy(selb[:, :], lcp("sel")))
            link(dve.tensor_copy(ident_b[:, :], ident))

            for b in range(1, 8, 2):
                dve.wait_ge(s_tri, b + 1)
                dve.tensor_copy(grid(tri[:, :])[:, :, 4 * b:4 * b + 4].rearrange("p j c -> p c j"),
                                ps[:, b, :].rearrange("p (c j) -> p c j", c=4)).then_inc(s_trd, 1)

            def sums(squares, done, at):
                def body(g, slot):
                    dve.wait_ge(squares, g + 1)
                    dve.tensor_reduce(ssum[:, bass.ds(g * JG, JG)], grid(gates[:, (at + slot) * W:(at + slot + 1) * W]),
                                      AX_X, ALU.add).then_inc(done, 1)
                return body
            groups(dve, sums(s_q4, s_v4, 0))
            dve.wait_ge(s_v4, G)
            dve.tensor_scalar(ssum, ssum, 1.0 / C, LN_EPS, ALU.mult, ALU.add).then_inc(s_var, 1)

            dve.wait_ge(s_brow, 5)
            link(dve.scalar_tensor_tensor(out=wexp[:, :], in0=lcp("expert_b"), scalar=1.0 / C, in1=ps[:, 7, 0:2 * C],
                                          op0=ALU.mult, op1=ALU.add))
            rv = rcm[:, :].rearrange("p (r f) -> p r f", f=C + E)
            link(dve.tensor_tensor(cb[:, :], ps[:, 4, P:P + C], lcp("out_b"), ALU.add))
            link(dve.tensor_copy(w4[:, 0:P], lcp("w4")[:, 0:P]))
            link(dve.tensor_copy(w4[:, P:2 * P], ps[:, 5, P:2 * P]))
            link(dve.tensor_copy(rv[:, :, 0:C], centre.rearrange("p (r c) -> p r c", c=C)))
            dve.tensor_copy(rv[:, :, C:C + E], ps[:, 6, 0:R * E].rearrange("p (r e) -> p r e", e=E)).then_inc(s_w4, 1)
            dve.wait_ge(s_std, 2)
            link(dve.reciprocal(rstd, std))

            def update(g, slot):
                dve.wait_ge(s_go, g + 1)
                wait(dve, s_x1, g - 1)
                dve.tensor_tensor(grid(sq[:, slot * W:(slot + 1) * W]),
                                  grid(ps[:, 5 + 2 * slot, :]),
                                  over(rstd[:, bass.ds(g * JG, JG)], JG, C), ALU.mult).then_inc(s_u1, 1)

            def close(g, slot):
                dve.wait_ge(s_u2, g + 1)
                dve.wait_ge(s_gs, g + 1)
                v = sq[:, slot * W:(slot + 1) * W]
                dve.tensor_tensor(v, v, gates[:, slot * W:(slot + 1) * W], ALU.mult).then_inc(s_u3, 1)
                dve.wait_ge(s_res, g + 1)
                dve.wait_ge(s_u3, g + 1)
                dve.tensor_tensor(x1[:, bass.ds(g * W, W)], v, xi[:, bass.ds(g * W, W)], ALU.add).then_inc(s_x1, 1)
            ahead(dve, update, close)

            groups(dve, sums(s_q5, s_v5, 2))
            dve.wait_ge(s_v5, G)
            normaliser(1.0 / C, LN_EPS, 3)
            dve.engine_nop().then_inc(s_rstd, 1)

            HN = N // 2

            def of(tile, n, inner=E):
                return tile[:, n * HN * inner:(n + 1) * HN * inner]

            def each(tile, n):
                return grid(of(tile, n), E)

            best, gap, p1, p2 = (pair[:, n * N:(n + 1) * N] for n in range(4))
            top = ssum
            first, rest, second = tk

            def candidates(values, largest, to, n):
                link(dve.tensor_reduce(of(largest, n, 1), each(values, n), AX_X, ALU.max))
                dve.tensor_tensor(each(to, n), each(values, n), over(of(largest, n, 1), HN, E),
                                  ALU.is_equal).then_inc(s_cand, 1)

            def pick(to, n, count):
                dve.wait_ge(s_rank, count)
                link(dve.tensor_reduce(of(top, n, 1), each(to, n), AX_X, ALU.max))
                link(dve.tensor_tensor(each(to, n), each(to, n), over(of(top, n, 1), HN, E), ALU.is_equal))

            for n in range(2):
                dve.wait_ge(s_logit, n + 1)
                candidates(logit, best, first, n)
            for n in range(2):
                pick(first, n, n + 1)
                link(dve.scalar_tensor_tensor(out=of(rest, n), in0=of(first, n), scalar=-1e30, in1=of(logit, n),
                                              op0=ALU.mult, op1=ALU.add))
                candidates(rest, gap, second, n)
            for n in range(2):
                dve.wait_ge(s_cand, 3 + n)
                dve.tensor_tensor(of(gap, n, 1), of(gap, n, 1), of(best, n, 1), ALU.subtract).then_inc(s_diff, 1)
            for n in range(2):
                pick(second, n, n + 3)
            for n in range(2):
                dve.wait_ge(s_prob, 2 * n + 2)
                link(dve.tensor_tensor(each(first, n), each(first, n), over(of(p1, n, 1), HN, E), ALU.mult))
                link(dve.tensor_tensor(each(second, n), each(second, n), over(of(p2, n, 1), HN, E), ALU.mult))
                dve.tensor_tensor(of(first, n), of(first, n), of(second, n), ALU.add).then_inc(s_rem, 1)
            for part in range(PARTS - 1):
                for n in range(2):
                    dve.wait_ge(s_part, 2 * part + n + 1)
                    dve.tensor_tensor(each(first, n), each(first, n), w3part(n, part), ALU.subtract).then_inc(s_rem, 1)

            def products(g, slot):
                wait(dve, s_y, g - 1)
                for r in range(R):
                    dve.wait_ge(s_xr, 4 * g + (r + 1))
                    for h in range(2):
                        n = 2 * r + h
                        dve.wait_ge(s_wb, 8 * g + (n + 1))
                        dve.tensor_tensor(prod(slot, n), ps[:, SPREAD[n % 4], :], xrep[:, r * W:(r + 1) * W],
                                          ALU.mult).then_inc(s_pr, 1)

            def add_x1(g, slot):
                dve.wait_ge(s_y, g + 1)
                wait(dve, s_bk, g - 1)
                dve.tensor_tensor(yF[:, slot * W:(slot + 1) * W], ps[:, 4 + slot, :],
                                  x1F[:, bass.ds(g * W, W)], ALU.add).then_inc(s_yf, 1)
            ahead(dve, products, add_x1)


_OUT = ((1, N, N, C), "float32")


def kernel(**inputs):
    import numpy as _np
    import concourse.bacc as _bacc
    from concourse import mybir as _mybir
    from concourse.bass_utils import run_bass_kernel_spmd as _run

    a = {k.replace("L0_conv_", "").replace("L0_ffn_", ""): _np.asarray(v) for k, v in inputs.items()}
    f32 = a["x"].dtype

    def blocks(m):
        out = _np.zeros((R, m.shape[0], R, m.shape[1]), f32)
        for r in range(R):
            out[r, :, r, :] = m
        return out.reshape(R * m.shape[0], R * m.shape[1])

    def rows(v, times=1):
        return _np.tile(v, times)[None, :].repeat(P, axis=0)

    def column(v):
        return _np.tile(v, R)[:, None]

    ident = _np.eye(P, dtype=f32)
    centre = blocks(_np.eye(C, dtype=f32) - _np.full((C, C), 1.0 / C, f32))
    part = _np.eye(P, PARTS, dtype=f32)
    sel = _np.zeros((R, PARTS, E, R, 2, R, C), f32)
    for r in range(R):
        for e in range(E):
            sel[r, :, e, r, e // R, e % R, :] = 1.0
    sel = _np.concatenate([sel.reshape(KW, -1), _np.zeros((P - KW, 2 * R * P), f32)])
    prio = rows(_np.arange(E, 0, -1).astype(f32))

    fields = {
        "w1": blocks(_np.concatenate([a["gate_w"].T, a["lrp_w"].T], axis=1)),
        "b1": blocks(_np.tile(_np.concatenate([a["gate_b"], a["lrp_b"]]), (C, 1))),
        "ln1_w": column(a["ln1_w"]), "ln1_b": column(a["ln1_b"]), "part": part, "ident": ident,
        "centre": centre, "mean": blocks(_np.full((C, C), 1.0 / C, f32)),
        "mask": a["Z_mask_row"][0].T,
        "w4": _np.concatenate([blocks(a["og_w"].T), blocks(a["op_w"].T)], axis=1),
        "router": blocks(a["router_w"]),
        "expert": a["expert_w"].reshape(2, R * C, C).transpose(1, 0, 2).reshape(P, 2 * C),
        "expert_b": a["expert_b"].reshape(2, R, 1, C).repeat(C, axis=2).transpose(1, 2, 0, 3).reshape(P, 2 * C),
        "ln2_w": column(a["ln2_w"]), "ln2_b": column(a["ln2_b"]),
        "og_b": rows(a["og_b"], R), "out_b": rows(a["out_bias"]), "router_b": rows(a["router_b"]),
        "sel": sel, "prio": prio,
    }
    x = a["x"][0]
    arrays = {
        "in_x_k": _np.ascontiguousarray(x.transpose(1, 0, 2)).reshape(N, N * C),
        "in_x_i": _np.ascontiguousarray(x).reshape(N, N * C),
        "in_early": _np.ascontiguousarray(_np.concatenate([fields[n] for n, _ in EARLY], axis=1)),
        "in_late": _np.ascontiguousarray(_np.concatenate([fields[n] for n, _ in LATE], axis=1)),
    }
    nc = _bacc.Bacc("TRN2", target_bir_lowering=False, num_devices=1)
    args = [nc.dram_tensor(n, v.shape, _mybir.dt.from_np(v.dtype), kind="ExternalInput").ap()
            for n, v in arrays.items()]
    out = nc.dram_tensor("out_0", (N, N * C), _mybir.dt.from_np(_np.dtype(_OUT[1])), kind="ExternalOutput").ap()
    bass_metaformer(nc, *args, out)
    r = _run(nc, [arrays], core_ids=[0])
    return r.results[0]["out_0"].reshape(_OUT[0])
```

```python
from contextlib import ExitStack

import concourse.bass as bass
from concourse import mybir

P = 128
N = 128
C = 32
E = 8
R = P // C
F1 = 4 * C
G = 8
JG = N // G
W = JG * C
CH = JG // R
PARTS = 3
KW = R * PARTS * E

WARM = 11
STAY_WARM = 11
SPREAD_WARM = 1

PIECES = [(0, 1), (1, 1), (2, 1), (3, 1), (4, 2), (6, 2)]
ROOTED = 4

GUESS = 0x5F3759DF - (1 << 22) - (1 << 31)
ITERATIONS = 3

LN_C_EPS = 1e-6
LN_EPS = 1e-5

ALU = mybir.AluOpType
ACT = mybir.ActivationFunctionType
F32 = mybir.dt.float32
BF16 = mybir.dt.bfloat16
I32 = mybir.dt.int32
AX_X = mybir.AxisListType.X

EARLY = [("w1", R * F1), ("b1", F1), ("ln1_w", 1), ("ln1_b", 1), ("centre", P), ("mean", P), ("ident", P)]
LATE = [("mask", N), ("w4", R * 2 * C), ("router", R * E), ("expert", 2 * C), ("expert_b", 2 * C),
        ("ln2_w", 1), ("ln2_b", 1), ("og_b", R * C), ("out_b", C), ("router_b", E), ("part", PARTS),
        ("sel", 2 * R * P), ("prio", E)]


def columns(parts):
    at, out = 0, {}
    for name, width in parts:
        out[name] = (at, width)
        at += width
    return out, at


def bass_metaformer(nc, x_k, x_i, early, late, out):
    ecol, EW = columns(EARLY)
    lcol, LW = columns(LATE)

    with ExitStack() as ctx:
        def sb(name, width, dt=F32):
            return ctx.enter_context(nc.sbuf_tensor(name, [P, width], dt))

        def sem(name):
            return ctx.enter_context(nc.semaphore(name))

        def grid(ap, inner=C):
            return ap.rearrange("p (j c) -> p j c", c=inner)

        ps = ctx.enter_context(nc.psum_tensor("ps", [P, 8, 512], F32))

        xk = sb("xk", N * C)
        xi = sb("xi", N * C)
        lr = sb("lr", 2 * C * N)
        tri = sb("tri", N * C)
        triF = sb("triF", N * C)
        x1 = xk
        x1F = lr[:, 0:N * C]
        x1c = lr[:, N * C:2 * N * C]
        early_sb = sb("early_sb", EW)
        late_sb = sb("late_sb", LW)
        ring = sb("ring", 4 * W)
        ering = ring[:, 0:2 * W]
        fring = ring[:, 2 * W:4 * W]
        gates = sb("gates", 4 * W)
        sq = sb("sq", 2 * W)
        stats = sb("stats", 4 * N)
        nmean, ssum, std, rstd = (stats[:, n * N:(n + 1) * N] for n in range(4))
        ones_b = sb("ones_b", P, BF16)
        warm = sb("warm", W, BF16)
        lnb = sb("lnb", P)
        lnb2 = sb("lnb2", P)
        w1in = sb("w1in", R * F1)
        wexp = sb("wexp", 2 * C)
        w1 = sb("w1m", R * F1)
        split_a = sb("split_a", R * C)
        split_b = sb("split_b", R * C)
        part_b = sb("part_b", R * C, BF16)
        bias4 = sb("bias4", R * C, BF16)
        w4 = sb("w4m", R * 2 * C)
        w4in = sb("w4in", R * 2 * C)
        cb = sb("cb", C)
        rcm = sb("rcm", R * (C + E))
        selb = sb("selb", 2 * R * P, BF16)
        logit = sb("logit", N * E)
        tk = [sb(f"tk{n}", N * E) for n in range(3)]
        pair = sb("pair", 4 * N)
        w3 = sb("w3", N * PARTS * E, BF16)
        w3F = sb("w3F", N * N // R, BF16)
        wcopy = sb("wcopy", 2 * W)

        def ecp(name):
            a, w = ecol[name]
            return early_sb[:, a:a + w]

        def lcp(name):
            a, w = lcol[name]
            return late_sb[:, a:a + w]

        ident = ecp("ident")
        mask = lcp("mask")
        centre = ecp("centre")

        s_early = sem("early_loaded")
        s_late = sem("late_loaded")
        s_xk = [sem(f"xk_loaded{n}") for n in range(len(PIECES))]
        s_xi = sem("xi_loaded")
        s_ones = sem("ones_ready")
        s_p2 = sem("second_norm_parameters_ready")
        s_dve = sem("dve_step")
        s_mean = sem("sums_ready")
        s_sum = sem("sum_ready")
        s_cent = [sem(f"centred{n}") for n in range(len(PIECES))]
        s_sq = sem("squares_ready")
        s_var = sem("variance_ready")
        s_std = sem("std_ready")
        s_lnb = sem("shift_ready")
        s_brow = sem("bias_row_ready")
        s_w1 = sem("w1_ready")
        s_xs = sem("scaled_ready")
        s_tp = sem("transposed")
        s_xT = sem("xT_ready")
        s_proj = sem("projected")
        s_gate = sem("gate_ready")
        s_gm = sem("masked_gate_ready")
        s_lr = sem("lr_ready")
        s_tri = sem("tri_bank_ready")
        s_trs = sem("tri_stored")
        s_trd = sem("tri_stored_by_vector")
        s_res = sem("residual_ready")
        s_t4 = sem("tri_transposed")
        s_f4 = sem("triF_ready")
        s_c4 = sem("tri_centred")
        s_q4 = sem("tri_squares_ready")
        s_v4 = sem("tri_sums_ready")
        s_w4 = sem("w4_ready")
        s_go = sem("gate_and_update_ready")
        s_gs = sem("out_gate_ready")
        s_u1 = sem("update_scaled")
        s_u2 = sem("update_shifted")
        s_u3 = sem("update_gated")
        s_x1 = sem("x1_ready")
        s_t5 = sem("x1_transposed")
        s_f5 = sem("x1F_ready")
        s_c5 = sem("x1_centred")
        s_q5 = sem("x1_squares_ready")
        s_v5 = sem("x1_sums_ready")
        s_cand, s_rank, s_diff, s_prob, s_rem, s_part = (
            [sem(f"{name}{n}") for n in range(2)] for name in
            ("candidates_marked", "candidates_ranked", "logit_difference_ready", "probabilities_ready",
             "remainder_ready", "part_ready"))
        s_xh = sem("xhat_ready")
        s_turned = sem("turned_for_experts")
        s_turns = sem("turns_copied")
        s_xr = [[sem(f"replicated{slot}_{r}") for r in range(R)] for slot in range(2)]
        s_wc = sem("spread_weights_copied")
        s_pp = sem("pool_products_ready")
        s_wb = sem("weights_spread")
        s_pr = sem("products_ready")
        s_y = sem("experts_summed")
        s_yf = sem("result_F_ready")
        s_bk = sem("result_transposed")
        s_o = sem("result_T_ready")
        s_out = sem("out_stored")
        s_rstd = sem("rstd_ready")
        s_pick2 = [sem(f"second_picked{n}") for n in range(2)]
        s_w2 = [sem(f"second_weighed{n}") for n in range(2)]

        block = ctx.enter_context(nc.Block())
        SPREAD = [2, 3, 6, 7]

        def prod(slot, n):
            return (tri, triF)[slot][:, n * W:(n + 1) * W]

        POOL_N = [0, 4]
        VECTOR_N = [n for n in range(2 * R) if n not in POOL_N]
        VECTOR_UP_TO = [sum(n <= 2 * r + 1 for n in VECTOR_N) for r in range(R)]
        POOL_UP_TO = [sum(n <= 2 * r + 1 for n in POOL_N) for r in range(R)]

        def xrep(g, r, groups=1):
            at = (2 * r + g % 2) * W
            return (xi, x1)[g // 2 % 2][:, at:at + groups * W]

        def replicated(g):
            return 16 * R * (g // 4 + 1)

        xF = ring

        TURNS = [("x", 0), ("x", 1), ("x", 2), ("x", 3), ("w", 0), ("w", 1), ("w", 2), ("w", 3),
                 ("x", 4), ("x", 5), ("x", 6), ("x", 7), ("w", 4), ("w", 5), ("w", 6), ("w", 7)]

        STEP_TURNS = [((("w", 2),), (("w", 3),)), ((("x", 4),), (("x", 5),)), ((("x", 6),), (("x", 7),)),
                      ((("w", 4), ("w", 5)), (("w", 6), ("w", 7)))]

        def turns_up_to(kind, g):
            return TURNS.index((kind, g)) + 1

        def w3part(n, part):
            return w3[:, :].rearrange("p (h j n e) -> p h j n e", h=2, n=PARTS, e=E)[:, n, :, part, :]

        yF = sq
        result_T = x1c
        ident_b = sb("ident_b", P, BF16)

        def wait(eng, semaphore, value):
            if not isinstance(value, int) or value > 0:
                eng.wait_ge(semaphore, value)

        def groups(eng, body):
            body(0, 0)
            body(1, 1)
            with eng.Fori(1, G // 2) as turn:
                body(turn * 2, 0)
                body(turn * 2 + 1, 1)

        def ahead(eng, first, then):
            first(0, 0)
            first(1, 1)
            then(0, 0)
            first(2, 0)
            then(1, 1)
            with eng.Fori(1, G // 2 - 1) as turn:
                first(turn * 2 + 1, 1)
                then(turn * 2, 0)
                first(turn * 2 + 2, 0)
                then(turn * 2 + 1, 1)
            first(G - 1, 1)
            then(G - 2, 0)
            then(G - 1, 1)

        def between(eng, start, before, first, after):
            start()
            with eng.Fori(1, G // 2 - 1) as turn:
                for n in range(2):
                    before(turn * 2 + n, n)
                    first(turn * 2 + (n + 1), 1 - n)
                    after(turn * 2 + n, n)
            before(G - 2, 0)
            first(G - 1, 1)
            after(G - 2, 0)
            before(G - 1, 1)
            after(G - 1, 1)

        HN = N // 2
        X1_LAG = 2

        def piece(tile, n, inner=1):
            g, count = PIECES[n]
            return tile[:, g * JG * inner:(g + count) * JG * inner]

        def squares(n):
            return piece(triF, n, C)

        def per_token(tile, n):
            return piece(tile, n).unsqueeze(2).broadcast_to([P, PIECES[n][1] * JG, C])

        def half(slot, p):
            b = 4 * slot + 2 * p
            return ps[:, b:b + 2, :].rearrange("p b (r f) -> p (b r) f", f=F1)

        @block.sync
        def _(sp):
            for n in range(len(PIECES)):
                sp.dma_start(piece(xk, n, C), piece(x_k, n, C)).then_inc(s_xk[n], 16)
                if n == 0:
                    sp.dma_start(early_sb[:, :], early).then_inc(s_early, 16)
            sp.dma_start(late_sb[:, :], late).then_inc(s_late, 16)
            sp.dma_start(xi[:, :], x_i).then_inc(s_xi, 16)

            for g in range(0, G, 2):
                sp.wait_ge(s_turns, turns_up_to("x", g + 1))
                for r in range(R):
                    if g >= 4:
                        sp.wait_ge(s_pr, len(VECTOR_N) * (g - 3) + VECTOR_UP_TO[r])
                        sp.wait_ge(s_pp, len(POOL_N) * (g - 3) + POOL_UP_TO[r])
                    to = xrep(g, r, groups=2)
                    for e in range(R):
                        sp.dma_start(to[C * e:C * e + C, :], xF[C * r:C * r + C, g % 4 * W:(g % 4 + 2) * W])\
                            .then_inc(s_xr[g // 2 % 2][r], 16)

            def store(g, slot):
                sp.wait_ge(s_o, g + 1)
                sp.dma_start(out[:, bass.ds(g * W, W)], result_T[:, bass.ds(g * W, W)]).then_inc(s_out, 16)
            groups(sp, store)
            sp.wait_ge(s_out, 16 * G)

        @block.gpsimd
        def _(pool):
            pool.memset(ones_b[:, :], 1.0).then_inc(s_ones, 1)
            pool.memset(warm[:, :], 1.0).then_inc(s_ones, 1)

            def centred(n):
                pool.wait_ge(s_mean, n)
                v = grid(piece(xk, n, C))
                pool.tensor_tensor(v, v, per_token(nmean, n), ALU.add).then_inc(s_cent[n], 1)

            def masked(g, slot, p):
                pool.wait_ge(s_gate, 2 * g + (p + 1))
                v = grid(gates[:, (2 * slot + p) * W:(2 * slot + p + 1) * W], 2 * C)
                m = mask[:, bass.ds(g * JG + 8 * p, 8)].unsqueeze(2).broadcast_to([P, 8, 2 * C])
                pool.tensor_tensor(v, v, m, ALU.mult).then_inc(s_gm, 1)

            centred(1)
            centred(2)
            centred(3)
            pool.wait_ge(s_late, 16)
            masked(0, 0, 0)
            centred(4)
            masked(0, 0, 1)
            masked(1, 1, 0)
            centred(5)
            masked(1, 1, 1)

            pool.tensor_scalar(w4in[:, :], lcp("w4"), lcp("ln2_w"), None, ALU.mult).then_inc(s_p2, 1)
            pool.tensor_copy(lnb2[:, :], lcp("ln2_b").broadcast_to([P, P])).then_inc(s_p2, 1)

            with pool.Fori(1, G // 2) as turn:
                for n in range(2):
                    for p in range(2):
                        masked(turn * 2 + n, n, p)

            pool.wait_ge(s_xi, 16)
            pool.wait_ge(s_trs, 4)
            pool.wait_ge(s_trd, 4)

            def residual(g, slot):
                pool.tensor_tensor(xi[:, bass.ds(g * W, W)], xi[:, bass.ds(g * W, W)],
                                   tri[:, bass.ds(g * W, W)], ALU.add).then_inc(s_res, 1)
            groups(pool, residual)

            def shifted(g, slot):
                pool.wait_ge(s_u1, g + 1)
                v = grid(sq[:, slot * W:(slot + 1) * W])
                pool.tensor_tensor(v, v, cb[:, :].unsqueeze(1).broadcast_to([P, JG, C]), ALU.add)\
                    .then_inc(s_u2, 1)
            groups(pool, shifted)

            def rank(n, at):
                v = grid(tk[at][:, n * HN * E:(n + 1) * HN * E], E)
                pool.wait_ge(s_cand[n], at // 2 + 1)
                pool.tensor_tensor(v, v, lcp("prio").unsqueeze(1).broadcast_to([P, HN, E]),
                                   ALU.mult).then_inc(s_rank[n], 1)

            def xhat(g):
                v = grid(x1c[:, g * W:(g + 1) * W])
                pool.tensor_tensor(v, v, rstd[:, g * JG:(g + 1) * JG].unsqueeze(2).broadcast_to([P, JG, C]),
                                   ALU.mult).then_inc(s_xh, 1)

            def second_weighed(n):
                v = grid(tk[2][:, n * HN * E:(n + 1) * HN * E], E)
                pool.wait_ge(s_pick2[n], 1)
                pool.wait_ge(s_prob[n], 1)
                pool.tensor_tensor(v, v, pair[:, 2 * N + n * HN:2 * N + (n + 1) * HN].unsqueeze(2)
                                   .broadcast_to([P, HN, E]), ALU.mult).then_inc(s_w2[n], 1)

            pool.wait_ge(s_rstd, 1)
            xhat(0)
            xhat(1)
            rank(0, 0)
            xhat(2)
            rank(0, 2)
            xhat(3)
            second_weighed(0)
            pool.wait_ge(s_rstd, 2)
            xhat(4)
            xhat(5)
            xhat(6)
            xhat(7)
            rank(1, 0)

            def products(g):
                wait(pool, s_y, g - 1)
                for a, n in enumerate(POOL_N):
                    pool.wait_ge(s_wc, len(POOL_N) * g + (a + 1))
                    pool.wait_ge(s_xr[g // 2 % 2][n // 2], replicated(g))
                    pool.tensor_tensor(prod(g % 2, n), wcopy[:, a * W:(a + 1) * W], xrep(g, n // 2),
                                       ALU.mult).then_inc(s_pp, 1)

            products(0)
            rank(1, 2)
            products(1)
            second_weighed(1)
            for g in range(2, G):
                products(g)

        @block.scalar
        def _(act):
            def square_piece(n):
                act.wait_ge(s_cent[n], 1)
                act.activation(squares(n), piece(xk, n, C), ACT.Square).then_inc(s_sq, 1)

            def root_piece(n):
                act.wait_ge(s_var, n + 1)
                act.activation(piece(std, n), piece(ssum, n), ACT.Sqrt).then_inc(s_std, 1)

            def evacuate(g, slot):
                act.wait_ge(s_tp, g + 1)
                act.activation(fring[:, slot * W:(slot + 1) * W], ps[:, 4 * slot, :], ACT.Copy, bias=1.0)\
                   .then_inc(s_xT, 1)

            act.wait_ge(s_ones, 1)
            act.activation(pair[:, 0:1], ones_b[:, 0:1], ACT.Sqrt)
            square_piece(0)
            act.wait_ge(s_early, 16)
            act.activation(w1in[:, :], ecp("w1"), ACT.Identity, scale=ecp("ln1_w")).then_inc(s_lnb, 1)
            act.activation(lnb[:, :], ecp("mean"), ACT.Identity, scale=ecp("ln1_b")).then_inc(s_lnb, 1)
            root_piece(0)
            square_piece(1)
            evacuate(0, 0)
            square_piece(2)
            root_piece(1)
            square_piece(3)
            root_piece(2)

            def gate(p):
                def body(g, slot):
                    act.wait_ge(s_proj, 2 * g + (p + 1))
                    act.activation(grid(gates[:, (2 * slot + p) * W:(2 * slot + p + 1) * W], 2 * C),
                                   half(slot, p)[:, :, 0:2 * C], ACT.Sigmoid).then_inc(s_gate, 1)
                return body

            def start():
                evacuate(1, 1)
                root_piece(3)
                gate(0)(0, 0)
                gate(1)(0, 0)
                gate(0)(1, 1)
                evacuate(2, 0)
                square_piece(4)
                gate(1)(1, 1)
                square_piece(5)
            between(act, start, gate(0), evacuate, gate(1))

            for b in range(0, 8, 2):
                act.wait_ge(s_tri, b + 1)
                act.activation(grid(tri[:, :])[:, :, 4 * b:4 * b + 4].rearrange("p j c -> p c j"),
                               ps[:, b, :].rearrange("p (c j) -> p c j", c=4), ACT.Copy).then_inc(s_trs, 1)

            def triF_copy(g, slot):
                act.wait_ge(s_t4, g + 1)
                act.activation(triF[:, bass.ds(g * W, W)], ps[:, slot, :], ACT.Copy).then_inc(s_f4, 1)

            def square4(g, slot):
                act.wait_ge(s_c4, g + 1)
                wait(act, s_v4, g - 1)
                act.activation(gates[:, slot * W:(slot + 1) * W], ps[:, 2 + slot, :], ACT.Square).then_inc(s_q4, 1)

            ahead(act, triF_copy, square4)

            def out_gate(g, slot):
                act.wait_ge(s_go, g + 1)
                if g < 2:
                    act.wait_ge(s_v4, G - 1 + g)
                wait(act, s_u3, g - 1)
                act.activation(grid(gates[:, slot * W:(slot + 1) * W]),
                               grid(ps[:, 4 + 2 * slot, :]),
                               ACT.Sigmoid).then_inc(s_gs, 1)

            def x1F_copy(g, slot):
                act.wait_ge(s_t5, g + 1)
                act.activation(x1F[:, g * W:(g + 1) * W], ps[:, slot, :], ACT.Copy).then_inc(s_f5, 1)

            rc = ps[:, 2:4, 0:2 * R * (C + E)].rearrange("p b (j f) -> p b j f", f=C + E)

            def square5(g, slot):
                act.wait_ge(s_c5, g + 1)
                act.activation(x1c[:, g * W:(g + 1) * W].rearrange("p (b j c) -> p b j c", b=2, c=C),
                               rc[:, :, :, 0:C], ACT.Copy)
                act.activation(logit[:, g * JG * E:(g + 1) * JG * E].rearrange("p (b j c) -> p b j c", b=2, c=E),
                               rc[:, :, :, C:C + E], ACT.Copy)
                wait(act, s_v5, g - 1)
                act.activation(gates[:, (2 + slot) * W:(3 + slot) * W].rearrange("p (b j c) -> p b j c", b=2, c=C),
                               rc[:, :, :, 0:C], ACT.Square).then_inc(s_q5, 1)

            for t in range(G + X1_LAG + 1):
                if t < G:
                    out_gate(t, t % 2)
                if X1_LAG <= t < G + X1_LAG:
                    x1F_copy(t - X1_LAG, (t - X1_LAG) % 2)
                if t > X1_LAG:
                    square5(t - X1_LAG - 1, (t - X1_LAG - 1) % 2)

            def probabilities(n):
                lo, hi = n * HN, (n + 1) * HN
                act.wait_ge(s_diff[n], 1)
                act.activation(pair[:, 2 * N + lo:2 * N + hi], pair[:, N + lo:N + hi], ACT.Sigmoid)\
                   .then_inc(s_prob[n], 1)
                act.activation(pair[:, 3 * N + lo:3 * N + hi], pair[:, N + lo:N + hi], ACT.Sigmoid,
                               scale=-1.0).then_inc(s_prob[n], 1)

            def round_part(n, part):
                act.wait_ge(s_rem[n], part + 1)
                act.activation(w3part(n, part), grid(tk[0][:, n * HN * E:(n + 1) * HN * E], E),
                               ACT.Copy).then_inc(s_part[n], 1)

            def turn_copy(kind, g):
                t = turns_up_to(kind, g)
                act.wait_ge(s_turned, t)
                bank = ps[:, (t - 1) % 2, :]
                if kind == "w":
                    act.activation(w3F[0:KW, g * W:(g + 1) * W], bank[0:KW, 0:W // 2].bitcast(BF16),
                                   ACT.Copy).then_inc(s_turns, 1)
                    return
                if g >= 4:
                    for r in range(R):
                        act.wait_ge(s_xr[g // 2 % 2][r], replicated(g - 4))
                act.activation(xF[:, g % 4 * W:(g % 4 + 1) * W], bank, ACT.Copy, bias=1.0).then_inc(s_turns, 1)

            def weights_copy(g, a):
                act.wait_ge(s_wb, 8 * g + (POOL_N[a] + 1))
                wait(act, s_pp, len(POOL_N) * g + (a + 1 - len(POOL_N)))
                act.activation(wcopy[:, a * W:(a + 1) * W], ps[:, SPREAD[POOL_N[a] % 4], :], ACT.Copy)\
                   .then_inc(s_wc, 1)

            def result(g, slot):
                act.wait_ge(s_bk, g + 1)
                act.activation(result_T[:, bass.ds(g * W, W)], ps[:, 4 + slot, :], ACT.Copy).then_inc(s_o, 1)

            def step(g, slot):
                for a in range(len(POOL_N)):
                    weights_copy(g, a)
                result(g - 2, slot)

            turn_copy("x", 0)
            turn_copy("x", 1)
            probabilities(0)
            turn_copy("x", 2)
            turn_copy("x", 3)
            for part in range(PARTS):
                round_part(0, part)
            turn_copy("w", 0)
            turn_copy("w", 1)
            ROUNDS = [(2, 0), (2, 1), (3, 0)]
            for g in range(4):
                for a in range(2):
                    weights_copy(g, a)
                    if (g, a) in ROUNDS:
                        round_part(1, ROUNDS.index((g, a)))
                    for kind, h in STEP_TURNS[g][a]:
                        turn_copy(kind, h)
                    if (g, a) == (0, 1):
                        probabilities(1)
                if g >= 2:
                    result(g - 2, g % 2)
            with act.Fori(2, G // 2) as turn:
                for n in range(2):
                    step(turn * 2 + n, n)
            result(G - 2, 0)
            result(G - 1, 1)

        @block.tensor
        def _(pe):
            def keep_warm(bank, count):
                for _ in range(count):
                    pe.matmul(ps[:, bank, :], ones_b[:, :], warm[:, :], start=True, stop=True)

            pe.wait_ge(s_ones, 2)
            keep_warm(6, WARM)

            pe.wait_ge(s_lnb, 2)
            pe.matmul(ps[:, 7, :], lnb[:, :], ecp("w1"), start=True, stop=False)
            pe.matmul(ps[:, 7, :], centre, w1in[:, :], start=False, stop=True).then_inc(s_brow, 1)

            def turn_x(g, slot):
                pe.wait_ge(s_xs, g + 1)
                wait(pe, s_lr, 2 * g - 3)
                for q in range(CH):
                    t = pe.transpose(ps[:, 4 * slot, q * P:(q + 1) * P],
                                     ering[:, slot * W + q * P:slot * W + (q + 1) * P], ident)
                t.then_inc(s_tp, 1)

            def project(p):
                def body(g, slot):
                    if p == 0:
                        pe.wait_ge(s_xT, g + 1)
                    else:
                        wait(pe, s_lr, 2 * g - 2)
                    for q in range(2 * p, 2 * p + 2):
                        m = pe.matmul(ps[:, 4 * slot + q, :], fring[:, slot * W + q * P:slot * W + (q + 1) * P],
                                      w1[:, :], start=True, stop=True)
                    m.then_inc(s_proj, 1)
                return body

            def start():
                turn_x(0, 0)
                pe.wait_ge(s_w1, 1)
                project(0)(0, 0)
                turn_x(1, 1)
                project(1)(0, 0)
                project(0)(1, 1)
                project(1)(1, 1)
                turn_x(2, 0)
            between(pe, start, project(0), turn_x, project(1))

            pe.wait_ge(s_p2, 2)
            pe.wait_ge(s_lr, 2 * G - 2)
            for to, left, right in ((ps[:, 3, 0:2 * P], lnb2[:, :], lcp("w4")),
                                    (ps[:, 3, 2 * P:4 * P], centre, w4in[:, :]),
                                    (ps[:, 2, 0:R * E], centre, lcp("router")),
                                    (ps[:, 2, R * E:R * E + 2 * C], centre, lcp("expert"))):
                pe.matmul(to, left, right, start=True, stop=True).then_inc(s_brow, 1)

            pe.wait_ge(s_lr, 2 * G)
            for c in range(C):
                if c == 8:
                    pe.wait_ge(s_w4, 1)
                m = pe.matmul(ps[:, c // 4, (c % 4) * N:(c % 4 + 1) * N], lr[:, c * N:(c + 1) * N],
                              lr[:, (C + c) * N:(C + c + 1) * N], start=True, stop=True)
                if c % 4 == 3:
                    m.then_inc(s_tri, 1)

            def turn_tri(g):
                for q in range(CH):
                    t = pe.transpose(ps[:, g % 2, q * P:(q + 1) * P], tri[:, g * W + q * P:g * W + (q + 1) * P],
                                     ident)
                t.then_inc(s_t4, 1)

            def centre_tri(g):
                pe.wait_ge(s_f4, g + 1)
                if g >= 2:
                    pe.wait_ge(s_q4, g - 1)
                for q in range(CH):
                    m = pe.matmul(ps[:, 2 + g % 2, q * P:(q + 1) * P], triF[:, g * W + q * P:g * W + (q + 1) * P],
                                  centre, start=True, stop=True)
                m.then_inc(s_c4, 1)

            pe.wait_ge(s_trs, 4)
            pe.wait_ge(s_trd, 4)
            turn_tri(0)
            for g in range(G):
                if g + 1 < G:
                    if g >= 1:
                        pe.wait_ge(s_f4, g)
                    turn_tri(g + 1)
                centre_tri(g)

            def gate_update(g):
                if g == 0:
                    pe.wait_ge(s_w4, 2)
                if g >= 2:
                    pe.wait_ge(s_gs, g - 1)
                    pe.wait_ge(s_u1, g - 1)
                for q in range(CH):
                    chunk = triF[:, g * W + q * P:g * W + (q + 1) * P]
                    cols = slice(q * P, (q + 1) * P)
                    pe.matmul(ps[:, 4 + 2 * (g % 2), cols], chunk, w4[:, 0:P], start=True, stop=False)
                    pe.matmul(ps[:, 4 + 2 * (g % 2), cols], ones_b[:, :], bias4[:, :], start=False, stop=True)
                    m = pe.matmul(ps[:, 5 + 2 * (g % 2), cols], chunk, w4[:, P:2 * P], start=True, stop=True)
                m.then_inc(s_go, 1)

            def turn_x1(g):
                pe.wait_ge(s_x1, g + 1)
                for q in range(CH):
                    t = pe.transpose(ps[:, g % 2, q * P:(q + 1) * P], x1[:, g * W + q * P:g * W + (q + 1) * P], ident)
                t.then_inc(s_t5, 1)

            def centre_x1(g):
                pe.wait_ge(s_f5, g + 1)
                wait(pe, s_q5, g)
                if g == 0:
                    pe.wait_ge(s_q4, G)
                for q in range(CH):
                    m = pe.matmul(ps[:, 2 + q // 2, (q % 2) * R * (C + E):(q % 2 + 1) * R * (C + E)],
                                  x1F[:, g * W + q * P:g * W + (q + 1) * P], rcm[:, :], start=True, stop=True)
                m.then_inc(s_c5, 1)

            for t in range(G + X1_LAG + 1):
                if t < G:
                    gate_update(t)
                if X1_LAG <= t < G + X1_LAG:
                    g = t - X1_LAG
                    wait(pe, s_f5, g - 1)
                    turn_x1(g)
                if t > X1_LAG:
                    centre_x1(t - X1_LAG - 1)

            def turn_to_F(kind, g):
                t = turns_up_to(kind, g)
                wait(pe, s_turns, t - 2)
                if kind == "x":
                    pe.wait_ge(s_xh, g + 1)
                else:
                    pe.wait_ge(s_part[g // (G // 2)], PARTS)
                bank = ps[:, (t - 1) % 2, :]
                for q in range(CH):
                    if kind == "x":
                        m = pe.transpose(bank[:, q * P:(q + 1) * P], x1c[:, g * W + q * P:g * W + (q + 1) * P], ident)
                    else:
                        n = g * CH + q
                        m = pe.transpose(bank[0:KW, q * P // 2:(q + 1) * P // 2].bitcast(BF16),
                                         w3[:, n * KW:(n + 1) * KW], ident_b[:, :])
                m.then_inc(s_turned, 1)

            def used_before(numbers, n):
                if n >= 4:
                    return sum(m <= n - 4 for m in numbers)
                return sum(m <= n + 4 for m in numbers) - len(numbers)

            def spread(g, slot, r):
                for h in range(2):
                    n = 2 * r + h
                    if (n + 4) % 8 in POOL_N:
                        wait(pe, s_wc, len(POOL_N) * g + used_before(POOL_N, n))
                    else:
                        wait(pe, s_pr, len(VECTOR_N) * g + used_before(VECTOR_N, n))
                    pe.matmul(ps[:, SPREAD[n % 4], :], selb[0:KW, n * P:(n + 1) * P],
                              w3F[0:KW, bass.ds(g * W, W)], start=True, stop=True).then_inc(s_wb, 1)
                    if isinstance(g, int) and g == 0:
                        keep_warm(5, SPREAD_WARM)

            def sum_experts(g, slot, h):
                if h == 0:
                    wait(pe, s_o, g - 1)
                    pe.wait_ge(s_pr, len(VECTOR_N) * (g + 1))
                    pe.wait_ge(s_pp, len(POOL_N) * (g + 1))
                for r in range(R):
                    m = pe.matmul(ps[C * r:C * r + C, 4 + slot, :], wexp[:, h * C:(h + 1) * C],
                                  prod(slot, 2 * r + h), start=(h == 0), stop=(h == 1))
                if h == 1:
                    m.then_inc(s_y, 1)

            def turn_back(g, slot):
                pe.wait_ge(s_yf, g + 1)
                for q in range(CH):
                    t = pe.transpose(ps[:, 4 + slot, q * P:(q + 1) * P],
                                     yF[:, slot * W + q * P:slot * W + (q + 1) * P], ident)
                t.then_inc(s_bk, 1)

            def step(g, slot, sums, backs, turns=((), ())):
                spread(g, slot, 0)
                spread(g, slot, 1)
                for kind, h in turns[0]:
                    turn_to_F(kind, h)
                if sums:
                    sum_experts(g - 1, 1 - slot, 0)
                spread(g, slot, 2)
                for kind, h in turns[1]:
                    turn_to_F(kind, h)
                if sums:
                    sum_experts(g - 1, 1 - slot, 1)
                spread(g, slot, 3)
                if backs:
                    turn_back(g - 2, slot)

            for kind, g in TURNS[:turns_up_to("x", 3)]:
                turn_to_F(kind, g)
            keep_warm(6, STAY_WARM)
            turn_to_F("w", 0)
            turn_to_F("w", 1)
            pe.wait_ge(s_q5, G)
            for g in range(4):
                pe.wait_ge(s_turns, turns_up_to("w", g))
                step(g, g % 2, g >= 1, g >= 2, STEP_TURNS[g])
            pe.wait_ge(s_turns, len(TURNS))
            with pe.Fori(2, G // 2) as turn:
                for n in range(2):
                    step(turn * 2 + n, n, True, True)
            sum_experts(G - 1, 1, 0)
            sum_experts(G - 1, 1, 1)
            turn_back(G - 2, 0)
            turn_back(G - 1, 1)

        @block.vector
        def _(dve):
            steps = [0]

            def link(ins):
                steps[0] += 1
                ins.then_inc(s_dve, 1)
                dve.wait_ge(s_dve, steps[0])

            last = [0, 0]

            def after(n):
                dve.wait_ge(s_dve, last[n])

            def mark(n, ins):
                steps[0] += 1
                ins.then_inc(s_dve, 1)
                last[n] = steps[0]

            def over(small, n, inner):
                return small.unsqueeze(2).broadcast_to([P, n, inner])

            def split_selected(value, other, part, to):
                sel = lcp("part")
                link(dve.tensor_copy(part, value))
                link(dve.tensor_scalar(other, part, sel[:, 0:1], None, ALU.mult))
                link(dve.tensor_tensor(value, value, part, ALU.subtract))
                link(dve.tensor_copy(part, value))
                link(dve.scalar_tensor_tensor(out=other, in0=part, scalar=sel[:, 1:2], in1=other,
                                              op0=ALU.mult, op1=ALU.add))
                link(dve.tensor_tensor(value, value, part, ALU.subtract))
                link(dve.tensor_copy(part, value))
                link(dve.scalar_tensor_tensor(out=to, in0=part, scalar=sel[:, 2:3], in1=other,
                                              op0=ALU.mult, op1=ALU.add))

            def sum_piece(n):
                dve.wait_ge(s_xk[n], 16)
                link(dve.tensor_reduce(piece(ssum, n), grid(piece(xk, n, C)), AX_X, ALU.add))
                if n == 0:
                    v = grid(piece(xk, 0, C))
                    dve.scalar_tensor_tensor(out=v, in0=per_token(ssum, 0), scalar=-1.0 / C, in1=v,
                                             op0=ALU.mult, op1=ALU.add).then_inc(s_cent[0], 1)
                else:
                    dve.tensor_scalar(piece(nmean, n), piece(ssum, n), -1.0 / C, None, ALU.mult).then_inc(s_mean, 1)

            def sum_squares(n):
                dve.wait_ge(s_sq, n + 1)
                dve.tensor_reduce(piece(ssum, n), grid(squares(n)), AX_X, ALU.add).then_inc(s_sum, 1)
                dve.wait_ge(s_sum, n + 1)
                part = 1.0 if n < ROOTED else 0.5
                m = dve.tensor_scalar(piece(ssum, n), piece(ssum, n), part * (1.0 + LN_EPS) / C,
                                      part * LN_C_EPS * LN_EPS, ALU.mult, ALU.add)
                if n < ROOTED:
                    m.then_inc(s_var, 1)
                else:
                    link(m)
                    guess(piece(rstd, n), piece(ssum, n))

            def normalise_piece(n):
                dve.wait_ge(s_std, n + 1)
                link(dve.reciprocal(piece(rstd, n), piece(std, n)))

            def guess(root, halved):
                link(dve.tensor_scalar(root.bitcast(I32), halved.bitcast(I32), -0.5, float(GUESS), ALU.mult, ALU.add))

            def refine(root, halved, temp):
                link(dve.tensor_tensor(temp, root, root, ALU.mult))
                link(dve.tensor_tensor(temp, temp, halved, ALU.mult))
                link(dve.scalar_tensor_tensor(out=root, in0=temp, scalar=-1.5, in1=root, op0=ALU.add, op1=ALU.mult))

            def refine_piece(n):
                refine(piece(rstd, n), piece(ssum, n), piece(std, n))

            def half_of(stat, n):
                return stat[:, n * HN:(n + 1) * HN]

            def tri_variance(n):
                link(dve.tensor_scalar(half_of(ssum, n), half_of(ssum, n), 0.5 / C, 0.5 * LN_EPS, ALU.mult, ALU.add))
                guess(half_of(rstd, n), half_of(ssum, n))

            def refine_half(n):
                refine(half_of(rstd, n), half_of(ssum, n), half_of(std, n))

            def scaled(g, slot):
                wait(dve, s_tp, g - 1)
                dve.tensor_tensor(grid(ering[:, slot * W:(slot + 1) * W]), grid(xk[:, :])[:, bass.ds(g * JG, JG), :],
                                  over(rstd[:, bass.ds(g * JG, JG)], JG, C), ALU.mult).then_inc(s_xs, 1)

            def gated_part(g, slot, p):
                dve.wait_ge(s_gm, 2 * g + (p + 1))
                dve.tensor_tensor(lr[:, :].rearrange("p (f i) -> p i f", i=N)[:, bass.ds(g * JG + 8 * p, 8), :],
                                  half(slot, p)[:, :, 2 * C:4 * C],
                                  grid(gates[:, (2 * slot + p) * W:(2 * slot + p + 1) * W], 2 * C),
                                  ALU.mult).then_inc(s_lr, 1)

            def gated(g, slot):
                gated_part(g, slot, 0)
                gated_part(g, slot, 1)

            def start():
                sum_piece(0)
                sum_squares(0)
                sum_piece(1)
                normalise_piece(0)
                scaled(0, 0)
                sum_piece(2)
                dve.wait_ge(s_brow, 1)
                dve.scalar_tensor_tensor(out=w1[:, :].rearrange("p (r f) -> p r f", f=F1),
                                         in0=ecp("b1").unsqueeze(1).broadcast_to([P, R, F1]), scalar=1.0 / P,
                                         in1=ps[:, 7, :].rearrange("p (r f) -> p r f", f=F1),
                                         op0=ALU.mult, op1=ALU.add).then_inc(s_w1, 1)
                sum_squares(1)
                sum_piece(3)
                normalise_piece(1)
                scaled(1, 1)
                sum_squares(2)
                sum_squares(3)
                sum_piece(4)
                normalise_piece(2)
                scaled(2, 0)
                sum_piece(5)
                normalise_piece(3)
                gated_part(0, 0, 0)
                scaled(3, 1)
                gated_part(0, 0, 1)
                sum_squares(4)
                gated_part(1, 1, 0)
                for _ in range(ITERATIONS):
                    refine_piece(4)
                scaled(4, 0)
                gated_part(1, 1, 1)
                sum_squares(5)
                gated(2, 0)
                scaled(5, 1)
                for _ in range(ITERATIONS):
                    refine_piece(5)
                gated(3, 1)
            start()
            for g in range(4, G):
                if g + 2 < G:
                    scaled(g + 2, g % 2)
                gated(g, g % 2)

            dve.wait_ge(s_brow, 5)
            rv = rcm[:, :].rearrange("p (r f) -> p r f", f=C + E)
            dve.tensor_copy(w4[:, 0:P], lcp("w4")[:, 0:P])
            dve.scalar_tensor_tensor(out=wexp[:, :], in0=lcp("expert_b"), scalar=1.0 / C,
                                     in1=ps[:, 2, R * E:R * E + 2 * C], op0=ALU.mult, op1=ALU.add)
            dve.tensor_tensor(cb[:, :], ps[:, 3, P:P + C], lcp("out_b"), ALU.add)
            dve.tensor_copy(w4[:, P:2 * P], ps[:, 3, 2 * P + P:2 * P + 2 * P])
            dve.tensor_copy(rv[:, :, 0:C], centre.rearrange("p (r c) -> p r c", c=C))
            link(dve.tensor_copy(rv[:, :, C:C + E], ps[:, 2, 0:R * E].rearrange("p (r e) -> p r e", e=E)))
            dve.engine_nop().then_inc(s_w4, 1)
            link(dve.tensor_copy(split_a[:, 0:R * C], lcp("og_b")))
            split_selected(split_a[:, 0:R * C], split_b[:, 0:R * C], part_b[:, 0:R * C], bias4[:, :])
            link(dve.tensor_copy(selb[:, :], lcp("sel")))
            dve.tensor_copy(ident_b[:, :], ident).then_inc(s_w4, 1)

            for b in range(1, 8, 2):
                dve.wait_ge(s_tri, b + 1)
                dve.tensor_copy(grid(tri[:, :])[:, :, 4 * b:4 * b + 4].rearrange("p j c -> p c j"),
                                ps[:, b, :].rearrange("p (c j) -> p c j", c=4)).then_inc(s_trd, 1)

            def sums(squares, done, at):
                def body(g, slot):
                    dve.wait_ge(squares, g + 1)
                    dve.tensor_reduce(ssum[:, bass.ds(g * JG, JG)],
                                      grid(gates[:, (at + slot) * W:(at + slot + 1) * W]),
                                      AX_X, ALU.add).then_inc(done, 1)
                return body
            for g in range(G // 2):
                sums(s_q4, s_v4, 0)(g, g % 2)
            dve.wait_ge(s_v4, G // 2)
            tri_variance(0)
            for g in range(G // 2, G):
                sums(s_q4, s_v4, 0)(g, g % 2)
                if g - G // 2 < ITERATIONS:
                    refine_half(0)
            dve.wait_ge(s_v4, G)
            tri_variance(1)

            def update(g, slot):
                dve.wait_ge(s_go, g + 1)
                wait(dve, s_x1, g - 1)
                dve.tensor_tensor(grid(sq[:, slot * W:(slot + 1) * W]),
                                  grid(ps[:, 5 + 2 * slot, :]),
                                  over(rstd[:, bass.ds(g * JG, JG)], JG, C), ALU.mult).then_inc(s_u1, 1)

            def close(g, slot):
                dve.wait_ge(s_u2, g + 1)
                dve.wait_ge(s_gs, g + 1)
                v = sq[:, slot * W:(slot + 1) * W]
                dve.tensor_tensor(v, v, gates[:, slot * W:(slot + 1) * W], ALU.mult).then_inc(s_u3, 1)
                dve.wait_ge(s_res, g + 1)
                dve.wait_ge(s_u3, g + 1)
                dve.tensor_tensor(x1[:, bass.ds(g * W, W)], v, xi[:, bass.ds(g * W, W)], ALU.add).then_inc(s_x1, 1)

            def sums5(g):
                sums(s_q5, s_v5, 2)(g, g % 2)

            def half_variance(n):
                dve.wait_ge(s_v5, (n + 1) * G // 2)
                mark(n, dve.tensor_scalar(half_of(ssum, n), half_of(ssum, n), 0.5 / C, 0.5 * LN_EPS,
                                          ALU.mult, ALU.add))

            def half_guess(n):
                after(n)
                mark(n, dve.tensor_scalar(half_of(rstd, n).bitcast(I32), half_of(ssum, n).bitcast(I32), -0.5,
                                          float(GUESS), ALU.mult, ALU.add))

            def refine_a(n):
                after(n)
                mark(n, dve.tensor_tensor(half_of(std, n), half_of(rstd, n), half_of(rstd, n), ALU.mult))

            def refine_b(n):
                after(n)
                mark(n, dve.tensor_tensor(half_of(std, n), half_of(std, n), half_of(ssum, n), ALU.mult))

            def refine_c(n, final=False):
                after(n)
                m = dve.scalar_tensor_tensor(out=half_of(rstd, n), in0=half_of(std, n), scalar=-1.5,
                                             in1=half_of(rstd, n), op0=ALU.add, op1=ALU.mult)
                if final:
                    m.then_inc(s_rstd, 1)
                else:
                    mark(n, m)

            def of(tile, n, inner=E):
                return tile[:, n * HN * inner:(n + 1) * HN * inner]

            def each(tile, n):
                return grid(of(tile, n), E)

            best, gap, _, p1 = (pair[:, n * N:(n + 1) * N] for n in range(4))
            top = ssum
            first, rest, second = tk

            def scale_logits(n):
                dve.wait_ge(s_rstd, n + 1)
                mark(n, dve.tensor_tensor(each(logit, n), each(logit, n), over(half_of(rstd, n), HN, E), ALU.mult))

            def bias_logits(n):
                after(n)
                mark(n, dve.tensor_tensor(each(logit, n), each(logit, n),
                                          lcp("router_b").unsqueeze(1).broadcast_to([P, HN, E]), ALU.add))

            def largest(values, to, n):
                after(n)
                mark(n, dve.tensor_reduce(of(to, n, 1), each(values, n), AX_X, ALU.max))

            def candidates(values, value, to, n):
                after(n)
                dve.tensor_tensor(each(to, n), each(values, n), over(of(value, n, 1), HN, E),
                                  ALU.is_equal).then_inc(s_cand[n], 1)

            def top_rank(to, n, count):
                dve.wait_ge(s_rank[n], count)
                mark(n, dve.tensor_reduce(of(top, n, 1), each(to, n), AX_X, ALU.max))

            def pick_first(n):
                after(n)
                mark(n, dve.tensor_tensor(each(first, n), each(first, n), over(of(top, n, 1), HN, E), ALU.is_equal))

            def pick_second(n):
                after(n)
                dve.tensor_tensor(each(second, n), each(second, n), over(of(top, n, 1), HN, E),
                                  ALU.is_equal).then_inc(s_pick2[n], 1)

            def without_first(n):
                after(n)
                mark(n, dve.scalar_tensor_tensor(out=of(rest, n), in0=of(first, n), scalar=-1e30, in1=of(logit, n),
                                                 op0=ALU.mult, op1=ALU.add))

            def difference(n):
                dve.wait_ge(s_cand[n], 2)
                dve.tensor_tensor(of(gap, n, 1), of(gap, n, 1), of(best, n, 1), ALU.subtract).then_inc(s_diff[n], 1)

            def weigh_first(n):
                dve.wait_ge(s_prob[n], 2)
                mark(n, dve.tensor_tensor(each(first, n), each(first, n), over(of(p1, n, 1), HN, E), ALU.mult))

            def add_second(n):
                after(n)
                dve.wait_ge(s_w2[n], 1)
                dve.tensor_tensor(of(first, n), of(first, n), of(second, n), ALU.add).then_inc(s_rem[n], 1)

            def remainder(n, part):
                dve.wait_ge(s_part[n], part + 1)
                dve.tensor_tensor(each(first, n), each(first, n), w3part(n, part), ALU.subtract).then_inc(s_rem[n], 1)

            def product(g, n):
                if n == VECTOR_N[0]:
                    wait(dve, s_y, g - 1)
                dve.wait_ge(s_xr[g // 2 % 2][n // 2], replicated(g))
                dve.wait_ge(s_wb, 8 * g + (n + 1))
                dve.tensor_tensor(prod(g % 2, n), ps[:, SPREAD[n % 4], :], xrep(g, n // 2),
                                  ALU.mult).then_inc(s_pr, 1)

            def add_x1(g, slot):
                dve.wait_ge(s_y, g + 1)
                wait(dve, s_bk, g - 1)
                dve.tensor_tensor(yF[:, slot * W:(slot + 1) * W], ps[:, 4 + slot, :],
                                  x1F[:, bass.ds(g * W, W)], ALU.add).then_inc(s_yf, 1)
            for t in range(G + 1):
                if t < G:
                    update(t, t % 2)
                if t > 0:
                    close(t - 1, (t - 1) % 2)
                if t < ITERATIONS:
                    refine_half(1)
                if X1_LAG + 1 < t < G:
                    sums5(t - X1_LAG - 2)
                if t == G - 1:
                    half_variance(0)
                    half_guess(0)
                    refine_a(0)
                    refine_b(0)
                    refine_c(0)
                    refine_a(0)
                    refine_b(0)
            refine_c(0)
            refine_a(0)
            sums5(G - 4)
            refine_b(0)
            refine_c(0, final=True)

            scale_logits(0)
            sums5(G - 3)
            bias_logits(0)
            largest(logit, best, 0)
            candidates(logit, best, first, 0)
            sums5(G - 2)
            top_rank(first, 0, 1)
            pick_first(0)
            without_first(0)
            sums5(G - 1)
            largest(rest, gap, 0)
            half_variance(1)
            candidates(rest, gap, second, 0)
            half_guess(1)
            difference(0)
            for k in range(ITERATIONS):
                refine_a(1)
                if k == 0:
                    top_rank(second, 0, 2)
                if k == 1:
                    pick_second(0)
                refine_b(1)
                if k == 2:
                    weigh_first(0)
                refine_c(1, final=(k == ITERATIONS - 1))
            add_second(0)
            scale_logits(1)
            remainder(0, 0)
            bias_logits(1)
            remainder(0, 1)
            largest(logit, best, 1)
            candidates(logit, best, first, 1)
            product(0, VECTOR_N[0])
            top_rank(first, 1, 1)
            product(0, VECTOR_N[1])
            pick_first(1)
            product(0, VECTOR_N[2])
            without_first(1)
            product(0, VECTOR_N[3])
            largest(rest, gap, 1)
            product(0, VECTOR_N[4])
            candidates(rest, gap, second, 1)
            product(0, VECTOR_N[5])
            difference(1)
            product(1, VECTOR_N[0])
            product(1, VECTOR_N[1])
            top_rank(second, 1, 2)
            product(1, VECTOR_N[2])
            pick_second(1)
            product(1, VECTOR_N[3])
            weigh_first(1)
            product(1, VECTOR_N[4])
            product(1, VECTOR_N[5])
            add_second(1)
            add_x1(0, 0)
            product(2, VECTOR_N[0])
            product(2, VECTOR_N[1])
            remainder(1, 0)
            product(2, VECTOR_N[2])
            product(2, VECTOR_N[3])
            remainder(1, 1)
            for n in VECTOR_N[4:]:
                product(2, n)
            for g in range(3, G):
                add_x1(g - 2, g % 2)
                for n in VECTOR_N:
                    product(g, n)
            add_x1(G - 2, 0)
            add_x1(G - 1, 1)


_OUT = ((1, N, N, C), "float32")


def kernel(**inputs):
    import numpy as _np
    import concourse.bacc as _bacc
    from concourse import mybir as _mybir
    from concourse.bass_utils import run_bass_kernel_spmd as _run

    a = {k.replace("L0_conv_", "").replace("L0_ffn_", ""): _np.asarray(v) for k, v in inputs.items()}
    f32 = a["x"].dtype

    def blocks(m):
        out = _np.zeros((R, m.shape[0], R, m.shape[1]), f32)
        for r in range(R):
            out[r, :, r, :] = m
        return out.reshape(R * m.shape[0], R * m.shape[1])

    def rows(v, times=1):
        return _np.tile(v, times)[None, :].repeat(P, axis=0)

    def column(v):
        return _np.tile(v, R)[:, None]

    ident = _np.eye(P, dtype=f32)
    centre = blocks(_np.eye(C, dtype=f32) - _np.full((C, C), 1.0 / C, f32))
    part = _np.eye(P, PARTS, dtype=f32)
    sel = _np.zeros((R, PARTS, E, R, 2, R, C), f32)
    for r in range(R):
        for e in range(E):
            sel[r, :, e, r, e // R, e % R, :] = 1.0
    sel = _np.concatenate([sel.reshape(KW, -1), _np.zeros((P - KW, 2 * R * P), f32)])
    prio = rows(_np.arange(E, 0, -1).astype(f32))

    fields = {
        "w1": blocks(_np.concatenate([a["gate_w"].T, a["lrp_w"].T], axis=1)),
        "b1": rows(_np.concatenate([a["gate_b"], a["lrp_b"]])),
        "ln1_w": column(a["ln1_w"]), "ln1_b": column(a["ln1_b"]), "part": part, "ident": ident,
        "centre": centre, "mean": blocks(_np.full((C, C), 1.0 / C, f32)),
        "mask": a["Z_mask_row"][0].T,
        "w4": _np.concatenate([blocks(a["og_w"].T), blocks(a["op_w"].T)], axis=1),
        "router": blocks(a["router_w"]),
        "expert": a["expert_w"].reshape(2, R * C, C).transpose(1, 0, 2).reshape(P, 2 * C),
        "expert_b": a["expert_b"].reshape(2, R, 1, C).repeat(C, axis=2).transpose(1, 2, 0, 3).reshape(P, 2 * C),
        "ln2_w": column(a["ln2_w"]), "ln2_b": column(a["ln2_b"]),
        "og_b": rows(a["og_b"], R), "out_b": rows(a["out_bias"]), "router_b": rows(a["router_b"]),
        "sel": sel, "prio": prio,
    }
    x = a["x"][0]
    arrays = {
        "in_x_k": _np.ascontiguousarray(x.transpose(1, 0, 2)).reshape(N, N * C),
        "in_x_i": _np.ascontiguousarray(x).reshape(N, N * C),
        "in_early": _np.ascontiguousarray(_np.concatenate([fields[n] for n, _ in EARLY], axis=1)),
        "in_late": _np.ascontiguousarray(_np.concatenate([fields[n] for n, _ in LATE], axis=1)),
    }
    nc = _bacc.Bacc("TRN2", target_bir_lowering=False, num_devices=1)
    args = [nc.dram_tensor(n, v.shape, _mybir.dt.from_np(v.dtype), kind="ExternalInput").ap()
            for n, v in arrays.items()]
    out = nc.dram_tensor("out_0", (N, N * C), _mybir.dt.from_np(_np.dtype(_OUT[1])), kind="ExternalOutput").ap()
    bass_metaformer(nc, *args, out)
    r = _run(nc, [arrays], core_ids=[0])
    return r.results[0]["out_0"].reshape(_OUT[0])
```
